# Optimizing a Trainium2 kernel written in Bass

```python
import numpy as np
import jax
import jax.numpy as jnp

def _softmax(x, axis=-1):
    return jax.nn.softmax(x, axis=axis)

def _gelu(x):
    return jax.nn.gelu(x, approximate=True)

def _silu(x):
    return jax.nn.silu(x)

def _sigmoid(x):
    return jax.nn.sigmoid(x)

def _layernorm(x, axis=-1, eps=1e-05):
    m = jnp.mean(x, axis=axis, keepdims=True)
    v = jnp.var(x, axis=axis, keepdims=True)
    return (x - m) / jnp.sqrt(v + eps)

def _scatter_add(tgt, idx, src, axis=0):
    return tgt.at[idx].add(src)

def _segment_sum(src, seg, n):
    return jax.ops.segment_sum(src, seg, n)
kernel_name = 'mk_adj_preln_d4_adj_r2_a19d5c'

def setup_inputs(seed: int=0):
    np.random.seed(seed)
    _w = jnp.asarray

    def _rec_inputs():
        import jax
        import jax.numpy as jnp
        _gk = jax.random.key(seed)
        x = -0.0001538 + 1 * jax.random.normal(jax.random.fold_in(_gk, 1), (64, 128, 384), jnp.float32)
        _a = jax.random.bernoulli(jax.random.fold_in(_gk, 2), 0.015625, (64, 128, 128))
        _a = jnp.logical_or(_a, jnp.swapaxes(_a, -1, -2))
        _a = jnp.logical_or(_a, jnp.eye(128, dtype=bool))
        _af = _a.astype(jnp.float32)
        _af = _af * jax.random.uniform(jax.random.fold_in(_gk, 3), (64, 128, 128), jnp.float32, 0.05, 0.999992)
        adj = _af
        return (x, adj)
    x, adj = _rec_inputs()

    def _L0_gnn_setup():
        import jax, jax.numpy as jnp
        import numpy as np
        B, N, D, H = (8, 512, 384, 12)
        HD = D // H

        def _split_heads(x):
            b, n, _ = x.shape
            return x.reshape(b, n, H, HD).transpose(0, 2, 1, 3)
        key = jax.random.key(seed)
        ks = jax.random.split(key, 10)
        input_graph = jax.random.normal(ks[0], (B, N, D), dtype=jnp.float32)
        u = jax.random.uniform(ks[1], (B, N, N), dtype=jnp.float32)
        keep = jax.random.uniform(ks[2], (B, N, N)) < 0.15
        adj = jnp.where(keep, u, 0.0)
        s = 1.0 / np.sqrt(D)
        Wq = jax.random.normal(ks[3], (D, D), dtype=jnp.float32) * s
        bq = jnp.zeros((D,), dtype=jnp.float32)
        Wk = jax.random.normal(ks[4], (D, D), dtype=jnp.float32) * s
        bk = jnp.zeros((D,), dtype=jnp.float32)
        Wv = jax.random.normal(ks[5], (D, D), dtype=jnp.float32) * s
        bv = jnp.zeros((D,), dtype=jnp.float32)
        beta = jnp.asarray(0.1, dtype=jnp.float32)
        return {'input_graph': input_graph, 'adj': adj, 'Wq': Wq, 'bq': bq, 'Wk': Wk, 'bk': bk, 'Wv': Wv, 'bv': bv, 'beta': beta}
    _L0_gnn_all = _L0_gnn_setup()
    _L0_gnn_in = {k: v for k, v in _L0_gnn_all.items() if k in ('Wq', 'bq', 'Wk', 'bk', 'Wv', 'bv', 'beta')}
    del _L0_gnn_all

    def _L1_gnn_setup():
        import jax, jax.numpy as jnp
        import numpy as np
        B, S, H, L = (32, 256, 384, 2)

        def _layer_norm(z, a, b, eps=0.001):
            mu = jnp.mean(z, axis=-1, keepdims=True)
            sigma = jnp.std(z, axis=-1, keepdims=True, ddof=1)
            return (z - mu) / (sigma + eps) * a + b
        key = jax.random.key(seed)
        ks = jax.random.split(key, 6)
        hidden_state = jax.random.normal(ks[0], (B, S, H), dtype=jnp.float32)
        adjacency_matrix = (jax.random.uniform(ks[1], (B, S, S)) < 0.2).astype(jnp.float32)
        W_left = 0.05 * jax.random.normal(ks[2], (L, H, H), dtype=jnp.float32)
        W_right = 0.05 * jax.random.normal(ks[3], (L, H, H), dtype=jnp.float32)
        W_lin = 0.05 * jax.random.normal(ks[4], (L, H, H), dtype=jnp.float32)
        b_lin = jnp.zeros((L, H), dtype=jnp.float32)
        ln_a = jnp.ones((L, H), dtype=jnp.float32)
        ln_b = jnp.zeros((L, H), dtype=jnp.float32)
        return {'hidden_state': hidden_state, 'adjacency_matrix': adjacency_matrix, 'W_left': W_left, 'W_right': W_right, 'W_lin': W_lin, 'b_lin': b_lin, 'ln_a': ln_a, 'ln_b': ln_b}
    _L1_gnn_all = _L1_gnn_setup()
    _L1_gnn_in = {k: v for k, v in _L1_gnn_all.items() if k in ('W_left', 'W_right', 'W_lin', 'b_lin', 'ln_a', 'ln_b')}
    del _L1_gnn_all

    def _L2_gnn_setup():
        import jax, jax.numpy as jnp
        import numpy as np
        B, L, H = (8, 1024, 384)
        LN_EPS = 1e-12
        key = jax.random.key(seed)
        ks = jax.random.split(key, 10)
        hidden_state = jax.random.normal(ks[0], (B, L, H), dtype=jnp.float32)
        adjacency = jax.random.randint(ks[1], (B, L, L), 0, 2).astype(jnp.float32)
        bound = 1.0 / np.sqrt(H)
        W_left = jax.random.normal(ks[2], (H, H), dtype=jnp.float32) * np.sqrt(2.0 / (H + H))
        b_left = jax.random.uniform(ks[3], (H,), minval=-bound, maxval=bound, dtype=jnp.float32)
        W_self = jax.random.normal(ks[4], (H, H), dtype=jnp.float32) * np.sqrt(2.0 / (H + H))
        b_self = jax.random.uniform(ks[5], (H,), minval=-bound, maxval=bound, dtype=jnp.float32)
        W_right = jax.random.normal(ks[6], (H, H), dtype=jnp.float32) * np.sqrt(2.0 / (H + H))
        b_right = jax.random.uniform(ks[7], (H,), minval=-bound, maxval=bound, dtype=jnp.float32)
        gamma = jnp.ones((H,), dtype=jnp.float32)
        beta = jnp.zeros((H,), dtype=jnp.float32)
        return {'hidden_state': hidden_state, 'adjacency': adjacency, 'W_left': W_left, 'b_left': b_left, 'W_self': W_self, 'b_self': b_self, 'W_right': W_right, 'b_right': b_right, 'gamma': gamma, 'beta': beta}
    _L2_gnn_all = _L2_gnn_setup()
    _L2_gnn_in = {k: v for k, v in _L2_gnn_all.items() if k in ('W_left', 'b_left', 'W_self', 'b_self', 'W_right', 'b_right', 'gamma', 'beta')}
    del _L2_gnn_all

    def _L3_gnn_setup():
        import jax, jax.numpy as jnp
        import numpy as np
        NUM_HEADS = 12
        HIDDEN = 384
        HEAD = HIDDEN // NUM_HEADS
        SCALE = HIDDEN ** (-0.5)
        key = jax.random.key(seed)
        ks = jax.random.split(key, 8)
        B, N = (16, 256)
        std = HIDDEN ** (-0.5)
        return {'x': jax.random.normal(ks[0], (B, N, HIDDEN), dtype=jnp.float32), 'encoding_bias': jax.random.normal(ks[1], (B, N, N), dtype=jnp.float32), 'Wq': jax.random.normal(ks[2], (HIDDEN, HIDDEN), dtype=jnp.float32) * std, 'Wk': jax.random.normal(ks[3], (HIDDEN, HIDDEN), dtype=jnp.float32) * std, 'Wv': jax.random.normal(ks[4], (HIDDEN, HIDDEN), dtype=jnp.float32) * std, 'bv': jax.random.normal(ks[5], (HIDDEN,), dtype=jnp.float32) * 0.01, 'Wo': jax.random.normal(ks[6], (HIDDEN, HIDDEN), dtype=jnp.float32) * std, 'bo': jax.random.normal(ks[7], (HIDDEN,), dtype=jnp.float32) * 0.01}
    _L3_gnn_all = _L3_gnn_setup()
    _L3_gnn_in = {k: v for k, v in _L3_gnn_all.items() if k in ('Wq', 'Wk', 'Wv', 'bv', 'Wo', 'bo')}
    del _L3_gnn_all
    return {'x': x, 'adj': adj, 'L0_gnn_Wq': _L0_gnn_in['Wq'], 'L0_gnn_bq': _L0_gnn_in['bq'], 'L0_gnn_Wk': _L0_gnn_in['Wk'], 'L0_gnn_bk': _L0_gnn_in['bk'], 'L0_gnn_Wv': _L0_gnn_in['Wv'], 'L0_gnn_bv': _L0_gnn_in['bv'], 'L0_gnn_beta': _L0_gnn_in['beta'], 'L1_gnn_W_left': _L1_gnn_in['W_left'], 'L1_gnn_W_right': _L1_gnn_in['W_right'], 'L1_gnn_W_lin': _L1_gnn_in['W_lin'], 'L1_gnn_b_lin': _L1_gnn_in['b_lin'], 'L1_gnn_ln_a': _L1_gnn_in['ln_a'], 'L1_gnn_ln_b': _L1_gnn_in['ln_b'], 'L2_gnn_W_left': _L2_gnn_in['W_left'], 'L2_gnn_b_left': _L2_gnn_in['b_left'], 'L2_gnn_W_self': _L2_gnn_in['W_self'], 'L2_gnn_b_self': _L2_gnn_in['b_self'], 'L2_gnn_W_right': _L2_gnn_in['W_right'], 'L2_gnn_b_right': _L2_gnn_in['b_right'], 'L2_gnn_gamma': _L2_gnn_in['gamma'], 'L2_gnn_beta': _L2_gnn_in['beta'], 'L3_gnn_Wq': _L3_gnn_in['Wq'], 'L3_gnn_Wk': _L3_gnn_in['Wk'], 'L3_gnn_Wv': _L3_gnn_in['Wv'], 'L3_gnn_bv': _L3_gnn_in['bv'], 'L3_gnn_Wo': _L3_gnn_in['Wo'], 'L3_gnn_bo': _L3_gnn_in['bo']}

def reference(x, adj, L0_gnn_Wq, L0_gnn_bq, L0_gnn_Wk, L0_gnn_bk, L0_gnn_Wv, L0_gnn_bv, L0_gnn_beta, L1_gnn_W_left, L1_gnn_W_right, L1_gnn_W_lin, L1_gnn_b_lin, L1_gnn_ln_a, L1_gnn_ln_b, L2_gnn_W_left, L2_gnn_b_left, L2_gnn_W_self, L2_gnn_b_self, L2_gnn_W_right, L2_gnn_b_right, L2_gnn_gamma, L2_gnn_beta, L3_gnn_Wq, L3_gnn_Wk, L3_gnn_Wv, L3_gnn_bv, L3_gnn_Wo, L3_gnn_bo):
    import jax
    import jax.numpy as jnp

    def _L0_gnn_ref(input_graph, adj, Wq, bq, Wk, bk, Wv, bv, beta):
        import jax, jax.numpy as jnp
        import numpy as np
        B, N, D, H = (8, 512, 384, 12)
        HD = D // H

        def _split_heads(x):
            b, n, _ = x.shape
            return x.reshape(b, n, H, HD).transpose(0, 2, 1, 3)
        q = _split_heads(input_graph @ Wq + bq)
        k = _split_heads(input_graph @ Wk + bk)
        v = _split_heads(input_graph @ Wv + bv)
        scores = jnp.einsum('bhqd,bhkd->bhqk', q, k) / jnp.sqrt(jnp.asarray(HD, input_graph.dtype))
        adj_e = adj[:, None, :, :]
        scores = scores + beta * adj_e
        scores = jnp.where(adj_e > 0, scores, jnp.asarray(-9000000000000000.0, scores.dtype))
        probs = jax.nn.softmax(scores, axis=-1)
        out = jnp.einsum('bhqk,bhkd->bhqd', probs, v)
        return out.transpose(0, 2, 1, 3).reshape(input_graph.shape[0], input_graph.shape[1], D)

    def _L1_gnn_ref(hidden_state, adjacency_matrix, W_left, W_right, W_lin, b_lin, ln_a, ln_b):
        import jax, jax.numpy as jnp
        import numpy as np
        B, S, H, L = (32, 256, 384, 2)

        def _layer_norm(z, a, b, eps=0.001):
            mu = jnp.mean(z, axis=-1, keepdims=True)
            sigma = jnp.std(z, axis=-1, keepdims=True, ddof=1)
            return (z - mu) / (sigma + eps) * a + b
        temper = float(np.sqrt(H))
        adj = adjacency_matrix
        adj_tri = jnp.triu(adj, k=1)
        diag_mask = jnp.triu(adj, k=0) - adj_tri
        h = hidden_state
        for l in range(L):
            m_left = jnp.einsum('bsh,oh->bso', h, W_left[l])
            m_right = jnp.einsum('bsh,oh->bso', h, W_right[l])
            u_left = jnp.einsum('bih,bjh->bij', h, m_left) / temper
            u_right = jnp.einsum('bih,bjh->bij', h, m_right) / temper
            u = u_left * adj_tri + u_left * diag_mask + u_right * jnp.swapaxes(adj_tri, 1, 2)
            delta_exp_u = jnp.exp(u) * adj
            attention = delta_exp_u / (jnp.sum(delta_exp_u, axis=2, keepdims=True) + 1e-10)
            h_lin = jnp.einsum('bsh,oh->bso', h, W_lin[l]) + b_lin[l]
            ctx = jnp.matmul(attention, h_lin)
            h = jax.nn.relu(_layer_norm(ctx, ln_a[l], ln_b[l]))
        return h

    def _L2_gnn_ref(hidden_state, adjacency, W_left, b_left, W_self, b_self, W_right, b_right, gamma, beta):
        import jax, jax.numpy as jnp
        import numpy as np
        B, L, H = (8, 1024, 384)
        LN_EPS = 1e-12
        h = hidden_state
        d = h.shape[-1]
        n = h.shape[1]
        u = jnp.einsum('bld,bmd->blm', h, h) / jnp.sqrt(jnp.asarray(d, h.dtype))
        p = jax.nn.softmax(u, axis=-1)
        delta = p * adjacency
        attn = delta / (jnp.sum(delta, axis=2, keepdims=True) + 1e-10)
        h_left = jnp.einsum('bld,ed->ble', h, W_left) + b_left
        h_self = jnp.einsum('bld,ed->ble', h, W_self) + b_self
        h_right = jnp.einsum('bld,ed->ble', h, W_right) + b_right
        i = jnp.arange(n)[:, None]
        j = jnp.arange(n)[None, :]
        attn_left = jnp.where(j > i, attn, 0.0)
        attn_right = jnp.where(j < i, attn, 0.0)
        diag_a = jnp.diagonal(attn, axis1=1, axis2=2)
        ctx = jnp.einsum('blm,bmd->bld', attn_left, h_left) + diag_a[..., None] * h_self + jnp.einsum('blm,bmd->bld', attn_right, h_right)
        mu = jnp.mean(ctx, axis=-1, keepdims=True)
        var = jnp.mean(jnp.square(ctx - mu), axis=-1, keepdims=True)
        o = (ctx - mu) / jnp.sqrt(var + LN_EPS) * gamma + beta
        return jax.nn.relu(o)

    def _L3_gnn_ref(x, encoding_bias, Wq, Wk, Wv, bv, Wo, bo):
        import jax, jax.numpy as jnp
        import numpy as np
        NUM_HEADS = 12
        HIDDEN = 384
        HEAD = HIDDEN // NUM_HEADS
        SCALE = HIDDEN ** (-0.5)
        B, N, _ = x.shape
        q = (x @ Wq.T).reshape(B, N, NUM_HEADS, HEAD)
        k = (x @ Wk.T).reshape(B, N, NUM_HEADS, HEAD)
        v = (x @ Wv.T + bv).reshape(B, N, NUM_HEADS, HEAD)
        a = jnp.einsum('bnhd,bmhd->bhnm', q, k) * SCALE + encoding_bias[:, None, :, :]
        pad_mask = jnp.all(a == 0, axis=-1)
        a = jnp.where(pad_mask[..., None], -jnp.inf, a)
        a = jax.nn.softmax(a, axis=-1)
        a = jnp.nan_to_num(a)
        o = jnp.einsum('bhnm,bmhd->bnhd', a, v).reshape(B, N, HIDDEN)
        return o @ Wo.T + bo
    h = jnp.maximum(_layernorm(x, axis=-1), 0.0)
    x = x + _L0_gnn_ref(h, adj, L0_gnn_Wq, L0_gnn_bq, L0_gnn_Wk, L0_gnn_bk, L0_gnn_Wv, L0_gnn_bv, L0_gnn_beta)
    h = jnp.maximum(_layernorm(x, axis=-1), 0.0)
    x = x + _L1_gnn_ref(h, adj, L1_gnn_W_left, L1_gnn_W_right, L1_gnn_W_lin, L1_gnn_b_lin, L1_gnn_ln_a, L1_gnn_ln_b)
    h = jnp.maximum(_layernorm(x, axis=-1), 0.0)
    x = x + _L2_gnn_ref(h, adj, L2_gnn_W_left, L2_gnn_b_left, L2_gnn_W_self, L2_gnn_b_self, L2_gnn_W_right, L2_gnn_b_right, L2_gnn_gamma, L2_gnn_beta)
    h = jnp.maximum(_layernorm(x, axis=-1), 0.0)
    x = x + _L3_gnn_ref(h, adj, L3_gnn_Wq, L3_gnn_Wk, L3_gnn_Wv, L3_gnn_bv, L3_gnn_Wo, L3_gnn_bo)
    return x

_drawn_inputs = setup_inputs


def setup_inputs(seed=0):
    import zlib

    import numpy as np

    out = dict(_drawn_inputs(seed))
    spreads = {'L0_gnn_bq': (0.0, 0.792),
     'L0_gnn_bk': (0.0, 2.0),
     'L0_gnn_bv': (0.0, 0.1),
     'L1_gnn_b_lin': (0.0, 0.1),
     'L1_gnn_ln_a': (1.0, 0.2),
     'L1_gnn_ln_b': (0.0, 0.1),
     'L2_gnn_gamma': (1.0, 0.2),
     'L2_gnn_beta': (0.0, 0.1)}
    factors = {'L1_gnn_W_right': 2.673,
     'L2_gnn_b_left': 35.748,
     'L2_gnn_b_self': 2.806,
     'L2_gnn_b_right': 31.904,
     'L3_gnn_Wq': 8.0,
     'L3_gnn_Wk': 8.0,
     'L3_gnn_bv': 8.0,
     'L3_gnn_bo': 8.0}
    for name, (base, spread) in spreads.items():
        noise = np.random.default_rng([zlib.crc32(name.encode()), seed]).standard_normal(out[name].shape)
        drawn = base * np.exp(spread * noise) if base else spread * noise
        out[name] = jnp.asarray(drawn.astype(out[name].dtype))
    for name, factor in factors.items():
        out[name] = (out[name] * factor).astype(out[name].dtype)
    return out
```

```python
from contextlib import ExitStack

import concourse.bass as bass
from concourse import mybir

F32 = mybir.dt.float32
F32R = mybir.dt.float32r
F16 = mybir.dt.float16
BF16 = mybir.dt.bfloat16
ALU = mybir.AluOpType
ACT = mybir.ActivationFunctionType
AX = mybir.AxisListType

P = 128
D = 384
C = D // P
H = 12
HD = D // H
HPC = P // HD
G = 4
SLOTS = 16
VS = HD + 2
LIFT = 2.0 ** 15
RING = 4
FIRST_HI_SLOTS, FIRST_LO_SLOTS = [4, 10, 11], [5, 10, 11]
NEXT_SLOTS = [4, 8, 13]


def due(value):
    return not isinstance(value, int) or value > 0


LAYER1_PLAN = dict(
    scores=[0, 4, 8, 12], weigh=[0, 4, 8, 12], exp=[1, 5, 9, 13], at=[2, 6, 10, 14], turn=[3, 7, 11, 15],
    atT_lo=[3, 7, 11, 15], context=[5, 9, 13, 17], cs=[6, 10, 14, 18],
    h=[8, 10, 12, 14], adj=5, right=6, stats=[0, 1, 2, 3], eps=3, apply=[6, 7, 8, 9],
    close=[3, 5], z=[6, 7, 8, 9], relu=[8, 9, 11, 12], x=[11, 12, 14, 15])
LAYER2_PLAN = dict(
    scores=[0, 4, 8, 12], exp=[0, 4, 8, 12], at=[1, 5, 9, 13], turn=[2, 6, 10, 14],
    atT=[3, 7, 11, 15], context=[4, 8, 12, 16], cs=[5, 9, 13, 17],
    h=[8, 10, 12, 14], stats=[0, 1, 2, 3], eps=4, apply=[6, 7, 8, 9],
    close=[3, 5], z=[6, 7, 8, 9], relu=[8, 9, 11, 12], x=[11, 12, 14, 15])


LAYER0_PLAN = dict(
    weigh=1, exp=1, turn=2, pt=2, pt_lo=3, values=4, close=[7, 11, 15, 19],
    h=[7, 9, 11, 13], h_lo=[8, 10, 12, 14], stats=[0, 1, 2, 3], eps=4, apply=[5, 6, 7, 8], bias=9, late=1)
LAYER3_PLAN = dict(
    weigh=1, exp=1, turn=2, pt=2, pt_lo=3, values=4, close=[7, 11, 15, 19],
    turn_out=[8, 12, 16, 20], out=[9, 13, 17, 21], oT_lo=[9, 13, 17, 21], y=[10, 14, 18, 22],
    h=[7, 10, 11, 14], h_lo=[8, 11, 12, 15], stats=[0, 1, 2, 3], eps=4, apply=[5, 6, 7, 8], late=1)


def due_in(n, slots):
    return [(slot // SLOTS, g) for g, slot in enumerate(slots) if slot % SLOTS == n]


def pipeline(eng, quads, iteration, start=2):
    for j in range(-1, start):
        iteration(j, j % 2)
    with eng.Fori(start, quads - 3, 2) as j:
        iteration(j, 0)
        iteration(j + 1, 1)
    for j in range(quads - 2, quads + 2):
        iteration(j, j % 2)


def is_last(q, quads):
    return isinstance(q, int) and q == quads - 1


def ring(buf, q):
    if isinstance(q, int):
        return buf[:, q % buf.shape[1], :, :]
    return buf[:, bass.ds(q % buf.shape[1], 1), :, :].rearrange("p a g d -> p (a g) d")


def quad_of(dram, q):
    v = dram.rearrange("(q g) p n -> q p g n", g=G)
    if isinstance(q, int):
        return v[q]
    return v[bass.ds(q, 1)].rearrange("a p g n -> p (a g) n")


def dmas(q, par):
    return 8 * q + (16 - 8 * par)


MOM_STEPS = 6


def moments(v, dve, stats_done, need, st, tmp, mean, var, step, q, sign=1):
    dve.wait_ge(stats_done, need)
    v.tensor_tensor(tmp[:, 0], st[:, :, 1], st[:, :, 4], ALU.add).then_inc(step, 1)
    v.tensor_tensor(tmp[:, 1], st[:, :, 1], st[:, :, 4], ALU.subtract).then_inc(step, 1)
    v.tensor_tensor(tmp[:, 2], st[:, :, 2], st[:, :, 5], ALU.add).then_inc(step, 1)
    dve.wait_ge(step, MOM_STEPS * q + 1)
    v.tensor_scalar(mean[:], tmp[:, 0], 0.5 * sign, None, ALU.mult).then_inc(step, 1)
    dve.wait_ge(step, MOM_STEPS * q + 2)
    v.scalar_tensor_tensor(out=tmp[:, 3], in0=tmp[:, 1], scalar=0.25, in1=tmp[:, 1], op0=ALU.mult, op1=ALU.mult)\
        .then_inc(step, 1)
    dve.wait_ge(step, MOM_STEPS * q + 5)
    v.scalar_tensor_tensor(out=var[:], in0=tmp[:, 2], scalar=1.0 / D, in1=tmp[:, 3], op0=ALU.mult, op1=ALU.add)\
        .then_inc(step, 1)
    dve.wait_ge(step, MOM_STEPS * q + MOM_STEPS)


class Weights:

    SHARED = 3

    def __init__(self, nc, ctx, matrices):
        self.nc, self.matrices = nc, matrices
        self.raw = ctx.enter_context(nc.sbuf_tensor("w_raw", [P, 2, C, D], F32))
        self.hi, self.lo = ([ctx.enter_context(nc.sbuf_tensor(f"w_{half}{i}", [P, C, D], F32R)) for i in range(self.SHARED)]
                            for half in ("hi", "lo"))
        self.landed = [ctx.enter_context(nc.semaphore(f"w_landed{i}")) for i in range(2)]
        self.hi_done, self.lo_done = (ctx.enter_context(nc.semaphore(f"w_{half}_done")) for half in ("hi", "lo"))

    def load(self, sp, m):
        if m >= len(self.matrices):
            return
        if m >= 2:
            sp.wait_ge(self.hi_done, m - 1)
            sp.wait_ge(self.lo_done, m - 1)
        sp.dma_start(self.raw[:, m % 2], self.matrices[m].rearrange("(c p) n -> p c n", p=P)).then_inc(self.landed[m % 2], 16)

    def split_hi(self, act, m, hi):
        if m >= len(self.matrices):
            return
        act.wait_ge(self.landed[m % 2], 16 * (m // 2 + 1))
        self.nc.scalar.activation(hi[:], self.raw[:, m % 2], ACT.Identity).then_inc(self.hi_done, 1)

    def split_lo(self, dve, m, hi, lo):
        if m >= len(self.matrices):
            return
        dve.wait_ge(self.hi_done, m + 1)
        self.nc.vector.tensor_tensor(lo[:], self.raw[:, m % 2], hi[:].bitcast(F32), ALU.subtract).then_inc(self.lo_done, 1)


class FirstQuad:

    def __init__(self, nc, ctx, sources):
        self.sources = sources
        self.buf = ctx.enter_context(nc.sbuf_tensor("first_quad", [P, G, D], F32))
        self.landed = ctx.enter_context(nc.semaphore("first_landed"))

    def load(self, sp, k):
        if k < len(self.sources) and self.sources[k] is not None:
            sp.dma_start(self.buf[:], quad_of(self.sources[k], 0)).then_inc(self.landed, 16)

    def wait(self, eng, k):
        eng.wait_ge(self.landed, 16 * sum(source is not None for source in self.sources[:k + 1]))


class Phase:

    def __init__(self, nc, ctx, name, quads, consts, x_in, x_out, adj, weights, first_matrix, first, matrices, norm=True,
                 h_in=None, ring_quads=RING):
        self.nc, self.ctx, self.name, self.quads = nc, ctx, name, quads
        self.ident = consts["ident"]
        self.consts = consts
        self.x_in, self.x_out, self.adj_in, self.h_in = x_in, x_out, adj, h_in
        self.sems = []
        self.norm = norm
        self.first, self.k = first
        self.weights, self.m0, self.M = weights, first_matrix, matrices
        own = range(weights.SHARED, matrices)
        self.w_hi = weights.hi + [self.sb(f"w_hi{m}", [P, C, D], F32R) for m in own]
        self.w_lo = weights.lo + [self.sb(f"w_lo{m}", [P, C, D], F32R) for m in own]
        self.ring_quads = ring_quads
        self.x = self.sb("x", [P, ring_quads, G, D], F32)
        self.adj = [self.sb(f"adj{i}", [P, G, P], F32) for i in range(2)]
        if norm:
            self.hn = [self.sb("hn", [P, G, D], F32)] * 2
            self.st = self.sb("st", [P, G, 6], F32)
            self.mom = self.sb("mom", [P, 4, G], F32)
            self.neg_mean, self.var = self.sb("neg_mean", [P, G], F32), self.sb("var", [P, G], F32)
            self.shift = self.sb("shift", [P, G], F32)
            self.ve = self.sb("ve", [P, G], F32)
            self.rstd = self.sb("rstd", [P, G], F32)
        else:
            self.hn = [self.first.buf, self.sb("hn1", [P, G, D], F32)]
        self.hT_hi = [self.sb(f"hT_hi{i}", [P, C, G * P], F32R) for i in range(2)]
        self.hT_lo = [self.sb(f"hT_lo{i}", [P, C, G * P], F32R) for i in range(2)]
        self.ps_t = self.ps("ps_t")
        self.ps_proj = [self.ps(f"ps_proj{i}") for i in range(2)]

        s = self.sem
        self.rows_in = s("rows_in")
        self.x_landed = [s(f"x_landed{i}") for i in range(2)]
        self.adj_landed = [s(f"adj_landed{i}") for i in range(2)]
        self.stored = [s(f"stored{i}") for i in range(2)]
        self.x_done = s("x_done")
        self.stats_done, self.mom_step = s("stats_done"), s("mom_step")
        self.var_ready, self.pow_done, self.rstd_ready = s("var_ready"), s("pow_done"), s("rstd_ready")
        self.hn_done = s("hn_done")
        self.hT_turned = s("hT_turned")
        self.hT_hi_done, self.hT_lo_done = s("hT_hi_done"), s("hT_lo_done")
        self.hT_acted = self.hT_hi_done
        self.proj_done = s("proj_done")
        if not norm:
            self.h_landed = [s(f"h_landed{i}") for i in range(2)]

    def sb(self, name, shape, dt):
        return self.ctx.enter_context(self.nc.sbuf_tensor(f"{self.name}_{name}", shape, dt))

    def ps(self, name):
        return self.ctx.enter_context(self.nc.psum_tensor(f"{self.name}_{name}", [P, 512], F32))

    def sem(self, name):
        s = self.ctx.enter_context(self.nc.semaphore(f"{self.name}_{name}"))
        self.sems.append(s)
        return s

    def clear_semaphores(self):
        with self.nc.Block() as block:
            @block.sync
            def _(sp):
                numbers = sorted(s.num for s in self.sems)
                while numbers:
                    first = last = numbers.pop(0)
                    while numbers and numbers[0] == last + 1:
                        last = numbers.pop(0)
                    sp.sem_clear(range(first, last + 1))

    def real(self, q):
        return not isinstance(q, int) or 0 <= q < self.quads

    def load_first(self, sp):
        for i in range(0 if self.m0 == 0 else self.weights.SHARED, self.M):
            self.weights.load(sp, self.m0 + i)

    def first_to_split(self, j, n, slots):
        if not isinstance(j, int) or n not in slots:
            return []
        i = slots.index(n)
        return [m for m in range(self.M) if (j, m) in ((-1, i), (0, self.weights.SHARED + i))
                and (self.m0 == 0 or m >= self.weights.SHARED)]

    def first_hi(self, act, j, n):
        for i in self.first_to_split(j, n, FIRST_HI_SLOTS):
            self.weights.split_hi(act, self.m0 + i, self.w_hi[i])

    def first_lo(self, dve, j, n):
        for i in self.first_to_split(j, n, FIRST_LO_SLOTS):
            self.weights.split_lo(dve, self.m0 + i, self.w_hi[i], self.w_lo[i])

    def wait_weights(self, pe, count):
        pe.wait_ge(self.weights.hi_done, self.m0 + count)
        pe.wait_ge(self.weights.lo_done, self.m0 + count)

    def x_of(self, q):
        return self.first.buf if isinstance(q, int) and q == 0 else ring(self.x, q)

    def load_first_quad(self, sp):
        if self.k == 0:
            self.first.load(sp, 0)

    def load_next(self, sp, j):
        m = self.m0 + self.M
        if isinstance(j, int) and j == self.quads - 2:
            self.weights.load(sp, m)
            self.weights.load(sp, m + 1)
        if isinstance(j, int) and j == self.quads - 1:
            sp.wait_ge(self.stored[0], 16)
            if not self.norm:
                sp.wait_ge(self.hT_turned, G * (self.quads - 1))
            self.first.load(sp, self.k + 1)
        if isinstance(j, int) and j == self.quads:
            self.weights.load(sp, m + 2)

    def next_hi(self, act, j, n):
        if isinstance(j, int) and j == self.quads and n in NEXT_SLOTS:
            i = NEXT_SLOTS.index(n)
            if i == 0:
                act.wait_ge(self.proj_done, self.TILES * self.quads)
            self.weights.split_hi(act, self.m0 + self.M + i, self.weights.hi[i])

    def next_lo(self, dve, j, n):
        if isinstance(j, int) and j == self.quads and n in NEXT_SLOTS:
            i = NEXT_SLOTS.index(n)
            if i == 0:
                dve.wait_ge(self.proj_done, self.TILES * self.quads)
            self.weights.split_lo(dve, self.m0 + self.M + i, self.weights.hi[i], self.weights.lo[i])

    def load_x(self, sp, q, par):
        if not self.real(q):
            return
        if not isinstance(q, int) or q >= self.ring_quads:
            sp.wait_ge(self.stored[par], dmas(q - self.ring_quads, par))
        if not isinstance(q, int) or q >= 2:
            sp.wait_ge(self.x_landed[par], dmas(q - 2, par))
        sp.dma_start(ring(self.x, q), quad_of(self.x_in, q)).then_inc(self.x_landed[par], 16)

    def store_x(self, sp, q, par):
        if not self.real(q):
            return
        if is_last(q, self.quads):
            self.store_graphs(sp, q, par, self.x_done, ring(self.x, q))
            return
        sp.wait_ge(self.x_done, G * (q + 1))
        sp.dma_start(quad_of(self.x_out, q), ring(self.x, q)).then_inc(self.stored[par], 16)

    def store_graphs(self, sp, q, par, done, quad):
        for g in range(G):
            sp.wait_ge(done, G * q + g + 1)
            sp.dma_start(quad_of(self.x_out, q)[:, g, :], quad[:, g, :]).then_inc(self.stored[par], 16)

    def wait_stores(self, sp):
        for par in range(2):
            last_graphs = G - 1 if par == (self.quads - 1) % 2 else 0
            sp.wait_ge(self.stored[par], 16 * (self.quads // 2 + last_graphs))

    def norm_stats(self, dve, q, par, g):
        if not (self.norm and self.real(q)):
            return
        if g == 0 and isinstance(q, int) and q == 0:
            self.first.wait(dve, self.k)
        elif g == 0:
            dve.wait_ge(self.x_landed[par], dmas(q, par))
        xg = self.x_of(q)[:, g, :]
        self.nc.vector.bn_stats(self.st[:, g, :], xg).then_inc(self.stats_done, 1)

    def norm_eps(self, dve, q):
        if not (self.norm and self.real(q)):
            return
        if due(q):
            dve.wait_ge(self.rstd_ready, q)
        moments(self.nc.vector, dve, self.stats_done, G * (q + 1), self.st, self.mom, self.neg_mean, self.var,
                self.mom_step, q, sign=-1)
        self.nc.vector.tensor_scalar(self.ve[:], self.var[:], 1e-5, None, ALU.add).then_inc(self.var_ready, 1)

    def norm_rstd(self, pool, q):
        if not (self.norm and self.real(q)):
            return
        pool.wait_ge(self.var_ready, q + 1)
        if due(G * q):
            pool.wait_ge(self.hn_done, G * q)
        self.nc.gpsimd.tensor_tensor(self.rstd[:], self.ve[:], self.consts["neg_half"][:, 0:G],
                                     ALU.pow).then_inc(self.pow_done, 1)
        pool.wait_ge(self.pow_done, q + 1)
        self.nc.gpsimd.tensor_tensor(self.shift[:], self.neg_mean[:], self.rstd[:], ALU.mult)\
            .then_inc(self.rstd_ready, 1)

    def norm_apply(self, act, q, g):
        if not (self.norm and self.real(q)):
            return
        if g == 0:
            act.wait_ge(self.rstd_ready, q + 1)
        if due(G * (q - 1) + g + 1):
            act.wait_ge(self.hT_turned, G * (q - 1) + g + 1)
        self.nc.scalar.activation(self.hn[0][:, g, :], self.x_of(q)[:, g, :], ACT.Identity,
                                  bias=self.shift[:, g:g + 1], scale=self.rstd[:, g:g + 1]).then_inc(self.hn_done, 1)

    def turn_h(self, pe, q, par, g):
        if not self.real(q):
            return
        if self.norm:
            pe.wait_ge(self.hn_done, G * q + g + 1)
        elif g == 0:
            pe.wait_ge(self.h_landed[par], dmas(q, par))
        bank = self.bank_of_h(q, g)
        if bank is self.ps_t:
            self.wait_ps_t_free(pe, q, 1 if isinstance(q, int) and q == 0 and g == 3 else g)
        for c in range(C):
            last = self.nc.tensor.transpose(bank[:, c * P:(c + 1) * P], self.hn[par][:, g, c * P:(c + 1) * P],
                                            self.ident[:])
        last.then_inc(self.hT_turned, 1)

    def bank_of_h(self, q, g):
        if isinstance(q, int) and q == 0 and g < 3:
            return [self.ps_t, *self.ps_proj][g]
        return self.ps_t

    def take_hT_hi(self, act, q, par, g):
        if not self.real(q):
            return
        act.wait_ge(self.hT_turned, G * q + g + 1)
        self.wait_hT_free(act, q, g)
        self.nc.scalar.activation(self.hT_hi[par][:, :, g * P:(g + 1) * P], chunks(self.bank_of_h(q, g)), ACT.Relu)\
            .then_inc(self.hT_hi_done, 1)

    def take_hT_lo(self, dve, q, par, g):
        if not self.real(q):
            return
        dve.wait_ge(self.hT_acted, G * q + g + 1)
        self.nc.vector.scalar_tensor_tensor(
            out=self.hT_lo[par][:, :, g * P:(g + 1) * P], in0=chunks(self.bank_of_h(q, g)), scalar=0.0,
            in1=self.hT_hi[par][:, :, g * P:(g + 1) * P].bitcast(F32), op0=ALU.max, op1=ALU.subtract)\
            .then_inc(self.hT_lo_done, 1)

    def wait_hT_free(self, eng, q, g):
        if due(self.TILES * (q - 1)):
            eng.wait_ge(self.proj_done, self.TILES * (q - 1))

    def project_turned(self, par, bank, m, oc, c):
        mm = self.nc.tensor.matmul
        hi, lo = (w[m][:, c, oc * P:(oc + 1) * P] for w in (self.w_hi, self.w_lo))
        mm(bank[:], hi, self.hT_hi[par][:, c, :], start=(c == 0), stop=False)
        mm(bank[:], hi, self.hT_lo[par][:, c, :], start=False, stop=False)
        return mm(bank[:], lo, self.hT_hi[par][:, c, :], start=False, stop=(c == C - 1))

    def project_rows(self, par, bank, m, g, c):
        mm = self.nc.tensor.matmul
        hi, lo = (h[par][:, c, g * P:(g + 1) * P] for h in (self.hT_hi, self.hT_lo))
        out = bank[:, 0:D]
        mm(out, hi, self.w_hi[m][:, c, :], start=(c == 0), stop=False)
        mm(out, hi, self.w_lo[m][:, c, :], start=False, stop=False)
        return mm(out, lo, self.w_hi[m][:, c, :], start=False, stop=(c == C - 1))


def chunks(bank):
    return bank[:, 0:D].rearrange("p (c n) -> p c n", c=C)


def graphs(bank):
    return bank[:].rearrange("p (g n) -> p g n", g=G)


def heads(t):
    return t.rearrange("p (h d) -> p h d", h=H)


def value_heads(v, g):
    return v[:, g, :].rearrange("p (h e) -> p h e", h=H)[:, :, 0:HD]


def over(ap, n, axis):
    v = ap.unsqueeze(axis)
    return v.broadcast_to([*v.shape[:axis], n, *v.shape[axis + 1:]])


def attention_phase(nc, ctx, name, quads, consts, x_in, x_out, adj, weights, m0, first, bv, bo=None, bq=None, bk=None,
                    beta=None, q_scale=1.0):
    masked = beta is not None
    TILES = 3 + 3 + G
    PIECES = TILES * C
    ph = Phase(nc, ctx, name, quads, consts, x_in, x_out, adj, weights, m0, first, 3 if masked else 4)
    ph.TILES = TILES
    sb, ps, sem, real = ph.sb, ph.ps, ph.sem, ph.real
    PLAN = LAYER0_PLAN if masked else LAYER3_PLAN
    UNITS = SLOTS

    ps_s = [ps(f"ps_s{i}") for i in range(2)]
    ps_pt = [ps(f"ps_pt{i}") for i in range(2)]
    ps_o = ps("ps_o")
    qT = [sb(f"qT{i}", [P, C, G * P], F32) for i in range(2)]
    kT = [sb(f"kT{i}", [P, C, G * P], F32) for i in range(2)]
    v_hi, v_mid, v_lo = ([sb(f"v_{part}{i}", [P, G, H * VS], BF16) for i in range(2)] for part in ("hi", "mid", "lo"))
    v32 = [sb(f"v32_{i}", [P, D], F32) for i in range(2)]
    v_rest = [sb(f"v_rest{i}", [P, D], F32) for i in range(2)]
    sc = [sb(f"sc{i}", [P, C, P], F32) for i in range(2)]
    pr = [sb(f"pr{i}", [P, C, P], F32) for i in range(2)]
    pt_hi, pt_lo = ([sb(f"pt_{part}{i}", [P, C, P], F16) for i in range(2)] for part in ("hi", "lo"))
    nm = [sb(f"nm{i}", [P, C], F32) for i in range(2)]
    rc = sb("rc", [P, H], F32)
    ob = sb("ob", [P, D], F32)
    bv_rows = sb("bv_rows", [P, D], F32)
    rows = [(bv_rows, bv)]
    if masked:
        bias = [sb(f"bias{i}", [P, G, P], F32) for i in range(2)]
        hole = sb("hole", [P, G, P], F32)
        beta_col = sb("beta_col", [P, 1], F32)
        b_cols = sb("b_cols", [P, 2, C], F32)
        bs_cols = sb("bs_cols", [P, 2, C], F32)
        cols = [(b_cols[:, 0], bq), (b_cols[:, 1], bk)]
        hole_ready, soft_ready, bias_ready = sem("hole_ready"), sem("soft_ready"), sem("bias_ready")
        bs_ready = sem("bs_ready")
    else:
        am = [sb(f"am{i}", [P, H], F32) for i in range(2)]
        rcm = sb("rcm", [P, H], F32)
        bo_rows = sb("bo_rows", [P, D], F32)
        rows.append((bo_rows, bo))
        oT_hi, oT_lo = sb("oT_hi", [P, C, P], F32R), sb("oT_lo", [P, C, P], F32R)
        rcm_ready, absmax_done = sem("rcm_ready"), sem("absmax_done")
        xb_done, oT_turned, oT_hi_done, oT_lo_done, y_made = (
            sem(n) for n in ("xb_done", "oT_turned", "oT_hi_done", "oT_lo_done", "y_made"))

    qk_taken = sem("qk_taken")
    v_taken = sem("v_taken")
    v_hi_done, v_rest_done, v_mid_done, v_lo_done = (
        sem(n) for n in ("v_hi_done", "v_rest_done", "v_mid_done", "v_lo_done"))
    scores_done, scores_taken, negmax_done = sem("scores_done"), sem("scores_taken"), sem("negmax_done")
    exp_done, pt_turned, pt_hi_done, pv_done = sem("exp_done"), sem("pt_turned"), sem("pt_hi_done"), sem("pv_done")
    pt_lo_done = sem("pt_lo_done")
    rc_ready, ob_ready = sem("rc_ready"), sem("ob_ready")

    if masked:
        def wait_ps_t_free(pe, q, g):
            if due(G * q + g):
                pe.wait_ge(ph.hT_hi_done, G * q + g)
            if due(G * q + g):
                pe.wait_ge(ph.hT_lo_done, G * q + g)
    else:
        def wait_ps_t_free(pe, q, g):
            if due(G * q + g):
                pe.wait_ge(ph.hT_hi_done, G * q + g)
            if due(G * q + g):
                pe.wait_ge(ph.hT_lo_done, G * q + g)
            if due(G * (q - 2) + outs_before(PLAN["h"][g])):
                pe.wait_ge(ph.x_done, G * (q - 2) + outs_before(PLAN["h"][g]))
    ph.wait_ps_t_free = wait_ps_t_free

    def pieces(n):
        return range(n * PIECES // SLOTS, (n + 1) * PIECES // SLOTS)

    TAKE = [[t for t in range(TILES) if C * t + C - 1 in pieces(n)] for n in range(SLOTS)]

    def outs_before(slot):
        return max(g + 1 - G * (out // SLOTS) - (G if out % SLOTS >= slot else 0) for g, out in enumerate(PLAN["out"]))

    def turns_before(q, g):
        slot = PLAN["turn_out"][g]
        count = G * (q + 2 + slot // SLOTS) + sum(h <= slot % SLOTS for h in PLAN["h"])
        return min(count, G * quads) if isinstance(q, int) else count

    ph.clear_semaphores()
    block = ctx.enter_context(nc.Block())

    def lagged(j, n, lag):
        return (j - 1, 1, n - lag) if n >= lag else (j - 2, 2, n - lag + UNITS)

    @block.sync
    def _(sp):
        ph.load_first_quad(sp)
        ph.load_x(sp, 0, 0)
        ph.load_first(sp)
        for dst, b in rows:
            sp.dma_start(dst[:], b.partition_broadcast(P)).then_inc(ph.rows_in, 16)
        if masked:
            for dst, b in cols:
                sp.dma_start(dst, b.rearrange("(c p) -> p c", p=P), allow_slow_non_contiguous=True).then_inc(ph.rows_in, 16)
            sp.dma_start(beta_col[:], beta.partition_broadcast(P)).then_inc(ph.rows_in, 16)

        def iteration(j, par):
            ph.store_x(sp, j - 2, par)
            ph.load_x(sp, j + 2, par)
            if real(j):
                if masked:
                    if due(j - 1):
                        sp.wait_ge(bias_ready, j - 1)
                else:
                    if due(UNITS * (j - 1)):
                        sp.wait_ge(scores_taken, UNITS * (j - 1))
                sp.dma_start(ph.adj[par][:], quad_of(adj, j)).then_inc(ph.adj_landed[par], 16)
            ph.load_next(sp, j)

        pipeline(sp, quads, iteration)
        ph.wait_stores(sp)

    @block.tensor
    def _(pe):

        def scores(q, back, par, n):
            if not real(q):
                return
            u, g, lo = UNITS * q + n, n // 4, HD * (n % 4)
            if n == 0:
                pe.wait_ge(qk_taken, 2 * C * (q + 1))
            if due(u - 1):
                pe.wait_ge(scores_taken, u - 1)
            for c in range(C):
                last = nc.tensor.matmul(ps_s[n % 2][:, c * P:(c + 1) * P], qT[par][lo:lo + HD, c, g * P:(g + 1) * P],
                                        kT[par][lo:lo + HD, c, g * P:(g + 1) * P], start=True, stop=True)
            last.then_inc(scores_done, 1)

        def project(j, par, k):
            if not real(j) or k >= PIECES:
                return
            t, c = k // C, k % C
            if k == 0:
                if isinstance(j, int) and j == 0:
                    ph.wait_weights(pe, 3)
                pe.wait_ge(ph.hT_hi_done, G * (j + 1))
                pe.wait_ge(ph.hT_lo_done, G * (j + 1))
            if c == 0:
                if t < 2:
                    if due(G * (j - 1) + 3 + t):
                        pe.wait_ge(v_taken, G * (j - 1) + 3 + t)
                elif t < 8:
                    pe.wait_ge(qk_taken, 2 * C * j + t - 1)
                else:
                    pe.wait_ge(v_taken, G * j + t - 7)
            bank = ph.ps_proj[t % 2]
            if t < 2 * C:
                last = ph.project_turned(par, bank, t % 2, t // 2, c)
            else:
                last = ph.project_rows(par, bank, 2, t - 2 * C, c)
            if c == C - 1:
                last.then_inc(ph.proj_done, 1)

        def turn_probs(q, n):
            if not real(q):
                return
            u = UNITS * q + n
            pe.wait_ge(exp_done, u + 1)
            if due(u - 1):
                pe.wait_ge(pt_lo_done, u - 1)
            for c in range(C):
                last = nc.tensor.transpose(ps_pt[n % 2][:, c * P:(c + 1) * P], pr[n % 2][:, c, :], ph.ident[:])
            last.then_inc(pt_turned, 1)

        def values(q, par, n):
            if not real(q):
                return
            u, g, r = UNITS * q + n, n // 4, n % 4
            pe.wait_ge(pt_hi_done, u + 1)
            pe.wait_ge(pt_lo_done, u + 1)
            if r == 0:
                pe.wait_ge(v_lo_done, G * q + g + 1)
            if r == 0:
                if due(G * q + g):
                    pe.wait_ge(ob_ready, G * q + g)
            for c in range(C):
                h = HPC * c + r
                mm, out = nc.tensor.matmul, ps_o[:, VS * h:VS * h + HD + 1]
                hi, mid, lo = (v[par][:, g, VS * h:VS * h + HD + 1] for v in (v_hi, v_mid, v_lo))
                mm(out, pt_hi[n % 2][:, c, :], hi, start=True, stop=False)
                mm(out, pt_hi[n % 2][:, c, :], mid, start=False, stop=False)
                mm(out, pt_hi[n % 2][:, c, :], lo, start=False, stop=False)
                mm(out, pt_lo[n % 2][:, c, :], hi, start=False, stop=False)
                last = mm(out, pt_lo[n % 2][:, c, :], mid, start=False, stop=True)
            last.then_inc(pv_done, 1)

        def turn_out(q, g):
            if not real(q):
                return
            pe.wait_ge(ob_ready, G * q + g + 1)
            if due(G * q + g):
                pe.wait_ge(ph.x_done, G * q + g)
            pe.wait_ge(ph.hT_lo_done, turns_before(q, g))
            for c in range(C):
                last = nc.tensor.transpose(ph.ps_t[:, c * P:(c + 1) * P], ob[:, c * P:(c + 1) * P], ph.ident[:])
            last.then_inc(oT_turned, 1)

        def project_out(q, g):
            if not real(q):
                return
            pe.wait_ge(oT_hi_done, G * q + g + 1)
            pe.wait_ge(oT_lo_done, G * q + g + 1)
            if isinstance(q, int) and q == 0 and g == 0:
                ph.wait_weights(pe, 4)
            mm, out = nc.tensor.matmul, ph.ps_t[:, 0:D]
            for c in range(C):
                mm(out, oT_hi[:, c, :], ph.w_hi[3][:, c, :], start=(c == 0), stop=False)
                mm(out, oT_hi[:, c, :], ph.w_lo[3][:, c, :], start=False, stop=False)
                last = mm(out, oT_lo[:, c, :], ph.w_hi[3][:, c, :], start=False, stop=(c == C - 1))
            last.then_inc(y_made, 1)

        def iteration(j, par):
            for n in range(SLOTS):
                scores(j - 1, 1, 1 - par, n)
                q, back, m = lagged(j, n, PLAN["values"])
                if m % 4 or not PLAN["late"]:
                    values(q, (par + back) % 2, m)
                for k in pieces(n):
                    project(j, par, k)
                if m % 4 == 0 and PLAN["late"]:
                    values(q, (par + back) % 2, m)
                for _, g in due_in(n, PLAN["h"]):
                    ph.turn_h(pe, j + 1, 1 - par, g)
                if not masked:
                    for back, g in due_in(n, PLAN["turn_out"]):
                        turn_out(j - 1 - back, g)
                    for back, g in due_in(n, PLAN["out"]):
                        project_out(j - 1 - back, g)
                q, _, m = lagged(j, n, PLAN["turn"])
                turn_probs(q, m)

        pipeline(pe, quads, iteration)

    @block.scalar
    def _(act):

        def take_qk(j, par, t):
            if not real(j):
                return
            oc, dst = t // 2, (qT, kT)[t % 2][par]
            act.wait_ge(ph.proj_done, TILES * j + t + 1)
            if t == 0:
                if due(UNITS * (j - 1)):
                    act.wait_ge(scores_done, UNITS * (j - 1))
            b = bs_cols[:, t % 2, oc:oc + 1] if masked else 0.0
            nc.scalar.activation(dst[:, oc, :], ph.ps_proj[t % 2][:], ACT.Identity, bias=b,
                                 scale=q_scale if t % 2 == 0 else 1.0).then_inc(qk_taken, 1)

        def exponentials(q, n):
            if not real(q):
                return
            u = UNITS * q + n
            act.wait_ge(negmax_done, u + 1)
            if due(u - 1):
                act.wait_ge(pt_turned, u - 1)
            for c in range(C):
                last = nc.scalar.activation(pr[n % 2][:, c, :], sc[n % 2][:, c, :], ACT.Exp,
                                            bias=nm[n % 2][:, c:c + 1])
            last.then_inc(exp_done, 1)

        def take_probs(q, n):
            if not real(q):
                return
            u = UNITS * q + n
            act.wait_ge(pt_turned, u + 1)
            if due(u - 1):
                act.wait_ge(pv_done, u - 1)
            nc.scalar.activation(pt_hi[n % 2][:], chunks(ps_pt[n % 2]), ACT.Identity, scale=LIFT).then_inc(pt_hi_done, 1)

        def take_v_hi(j, par, g):
            if not real(j):
                return
            act.wait_ge(v_taken, G * j + g + 1)
            if g == 0:
                if due(UNITS * (j - 1)):
                    act.wait_ge(pv_done, UNITS * (j - 1))
            nc.scalar.activation(value_heads(v_hi[par], g), heads(v32[g % 2][:]), ACT.Identity).then_inc(v_hi_done, 1)

        def take_v_mid(j, par, g):
            if not real(j):
                return
            act.wait_ge(v_rest_done, G * j + g + 1)
            nc.scalar.activation(value_heads(v_mid[par], g), heads(v_rest[g % 2][:]), ACT.Identity).then_inc(v_mid_done, 1)

        def take_oT_hi(q, g):
            if not real(q):
                return
            act.wait_ge(oT_turned, G * q + g + 1)
            if due(G * q + g):
                act.wait_ge(y_made, G * q + g)
            nc.scalar.activation(oT_hi[:], chunks(ph.ps_t), ACT.Identity).then_inc(oT_hi_done, 1)

        def iteration(j, par):
            if masked and isinstance(j, int) and j == 0:
                act.wait_ge(bs_ready, 1)
            for n in range(SLOTS):
                ph.first_hi(act, j, n)
                ph.next_hi(act, j, n)
                q, _, m = lagged(j, n, PLAN["exp"])
                exponentials(q, m)
                for t in TAKE[n]:
                    if t < 2 * C:
                        take_qk(j, par, t)
                    else:
                        take_v_hi(j, par, t - 2 * C)
                        if t > 2 * C:
                            take_v_mid(j, par, t - 2 * C - 1)
                if n == 0:
                    take_v_mid(j - 1, 1 - par, G - 1)
                for _, g in due_in(n, PLAN["apply"]):
                    ph.norm_apply(act, j + 1, g)
                for _, g in due_in(n, PLAN["h"]):
                    ph.take_hT_hi(act, j + 1, 1 - par, g)
                if not masked:
                    for back, g in due_in(n, PLAN["turn_out"]):
                        take_oT_hi(j - 1 - back, g)
                q, _, m = lagged(j, n, PLAN["pt"])
                take_probs(q, m)

        pipeline(act, quads, iteration)

    @block.vector
    def _(dve):
        def prepare():
            for i in range(2):
                nc.vector.memset(v_hi[i][:], 1.0)
                nc.vector.memset(v_mid[i][:], 0.0)
                nc.vector.memset(v_lo[i][:], 0.0)
            dve.wait_ge(ph.rows_in, 16 * (5 - 1) if masked else 32)
            if masked:
                for i, scale in enumerate((q_scale, 1.0)):
                    last = nc.vector.tensor_scalar(bs_cols[:, i], b_cols[:, i], scale, None, ALU.mult)
                last.then_inc(bs_ready, 1)

        def bias_scores(q, back, par, n):
            if not real(q):
                return
            u, g = UNITS * q + n, n // 4
            if n == 0:
                if masked:
                    dve.wait_ge(bias_ready, q + 1)
                else:
                    dve.wait_ge(ph.adj_landed[par], dmas(q, par))
            dve.wait_ge(scores_done, u + 1)
            if due(u - 1):
                dve.wait_ge(exp_done, u - 1)
            b = (bias[par] if masked else ph.adj[par])[:, g, :]
            nc.vector.tensor_tensor(sc[n % 2][:], chunks(ps_s[n % 2]), over(b, C, 1), ALU.add)\
                .then_inc(scores_taken, 1)
            dve.wait_ge(scores_taken, u + 1)
            nc.vector.tensor_reduce(nm[n % 2][:], sc[n % 2][:], AX.X, ALU.max, negate=True)\
                .then_inc(negmax_done, 1)
            if not masked:
                heads_of_unit = am[g % 2][:].rearrange("p (c r) -> p c r", r=HPC)[:, :, n % 4]
                nc.vector.tensor_reduce(heads_of_unit, sc[n % 2][:], AX.X, ALU.max, apply_absolute_value=True)\
                    .then_inc(absmax_done, 1)

        def take_v(j, par, g):
            if not real(j):
                return
            t = 2 * C + g
            dve.wait_ge(ph.proj_done, TILES * j + t + 1)
            if due(G * j + g - 1):
                dve.wait_ge(v_rest_done, G * j + g - 1)
            nc.vector.tensor_tensor(v32[g % 2][:], ph.ps_proj[t % 2][:, 0:D], bv_rows[:], ALU.add).then_inc(v_taken, 1)

        def take_probs_lo(q, n):
            if not real(q):
                return
            u = UNITS * q + n
            dve.wait_ge(pt_hi_done, u + 1)
            nc.vector.scalar_tensor_tensor(out=pt_lo[n % 2][:], in0=chunks(ps_pt[n % 2]), scalar=LIFT,
                                           in1=pt_hi[n % 2][:], op0=ALU.mult, op1=ALU.subtract).then_inc(pt_lo_done, 1)

        def close(q, par, g):
            if not real(q):
                return
            e = G * q + g
            dve.wait_ge(pv_done, UNITS * q + 4 * g + 4)
            o = ps_o[:, 0:H * VS].rearrange("p (h e) -> p h e", h=H)
            nc.vector.reciprocal(rc[:], o[:, :, HD]).then_inc(rc_ready, 1)
            dve.wait_ge(rc_ready, e + 1)
            inv = rc
            if not masked:
                dve.wait_ge(absmax_done, UNITS * q + 4 * g + 4)
                nc.vector.scalar_tensor_tensor(out=rcm[:], in0=am[g % 2][:], scalar=0.0, in1=rc[:],
                                               op0=ALU.is_gt, op1=ALU.mult).then_inc(rcm_ready, 1)
                dve.wait_ge(rcm_ready, e + 1)
                if due(e):
                    dve.wait_ge(oT_turned, e)
                inv = rcm
            nc.vector.tensor_tensor(heads(ob[:]), o[:, :, 0:HD], over(inv[:], HD, 2), ALU.mult)\
                .then_inc(ob_ready, 1)
            if masked:
                dve.wait_ge(ob_ready, e + 1)
                if isinstance(q, int) and q == 0 and g == 0:
                    dve.wait_ge(ph.x_landed[0], 16)
                xg = ring(ph.x, q)[:, g, :]
                nc.vector.tensor_tensor(xg, ob[:], xg, ALU.add).then_inc(ph.x_done, 1)

        def take_oT_lo(q, g):
            if not real(q):
                return
            dve.wait_ge(oT_hi_done, G * q + g + 1)
            nc.vector.tensor_tensor(oT_lo[:], chunks(ph.ps_t), oT_hi[:].bitcast(F32), ALU.subtract)\
                .then_inc(oT_lo_done, 1)

        def take_y(q, g):
            if not real(q):
                return
            dve.wait_ge(y_made, G * q + g + 1)
            dve.wait_ge(xb_done, G * q + g + 1)
            xg = ring(ph.x, q)[:, g, :]
            nc.vector.tensor_tensor(xg, ph.ps_t[:, 0:D], xg, ALU.add).then_inc(ph.x_done, 1)

        def make_bias(j, par):
            if not real(j):
                return
            dve.wait_ge(ph.adj_landed[par], dmas(j, par))
            nc.vector.tensor_scalar(hole[:], ph.adj[par][:], 0.0, -9e15, ALU.is_le, ALU.mult).then_inc(hole_ready, 1)
            nc.vector.tensor_scalar(bias[par][:], ph.adj[par][:], 0.0, beta_col[:, 0:1], ALU.max, ALU.mult)\
                .then_inc(soft_ready, 1)
            dve.wait_ge(hole_ready, j + 1)
            dve.wait_ge(soft_ready, j + 1)
            nc.vector.tensor_tensor(bias[par][:], bias[par][:], hole[:], ALU.add).then_inc(bias_ready, 1)

        def iteration(j, par):
            if isinstance(j, int) and j == 0:
                prepare()
            for n in range(SLOTS):
                ph.first_lo(dve, j, n)
                ph.next_lo(dve, j, n)
                q, back, m = lagged(j, n, PLAN["weigh"])
                bias_scores(q, back, (par + back) % 2, m)
                if not masked:
                    for back, g in due_in(n, PLAN["oT_lo"]):
                        take_oT_lo(j - 1 - back, g)
                    for back, g in due_in(n, PLAN["y"]):
                        take_y(j - 1 - back, g)
                for _, g in due_in(n, PLAN["h_lo"]):
                    ph.take_hT_lo(dve, j + 1, 1 - par, g)
                for back, g in due_in(n, PLAN["close"]):
                    close(j - 1 - back, (par + 1 + back) % 2, g)
                q, _, m = lagged(j, n, PLAN["pt_lo"])
                take_probs_lo(q, m)
                for t in TAKE[n]:
                    if t >= 2 * C:
                        take_v(j, par, t - 2 * C)
                for _, g in due_in(n, PLAN["stats"]):
                    ph.norm_stats(dve, j + 1, 1 - par, g)
                if n == PLAN["eps"]:
                    ph.norm_eps(dve, j + 1)
                if masked and n == PLAN["bias"]:
                    make_bias(j, par)

        pipeline(dve, quads, iteration)

    @block.gpsimd
    def _(pool):
        def split_v(j, par, g):
            if not real(j):
                return
            e = G * j + g
            pool.wait_ge(v_hi_done, e + 1)
            if due(e - 1):
                pool.wait_ge(v_lo_done, e - 1)
            nc.gpsimd.tensor_tensor(heads(v_rest[g % 2][:]), heads(v32[g % 2][:]), value_heads(v_hi[par], g), ALU.subtract)\
                .then_inc(v_rest_done, 1)

        def take_v_lo(j, par, g):
            if not real(j):
                return
            pool.wait_ge(v_mid_done, G * j + g + 1)
            nc.gpsimd.tensor_tensor(value_heads(v_lo[par], g), heads(v_rest[g % 2][:]), value_heads(v_mid[par], g),
                                    ALU.subtract).then_inc(v_lo_done, 1)

        def iteration(j, par):
            if not masked and isinstance(j, int) and j == 0:
                pool.wait_ge(ph.rows_in, 32)
                pool.wait_ge(ph.x_landed[0], 16)
            for n in range(SLOTS):
                if n == PLAN["eps"]:
                    ph.norm_rstd(pool, j + 1)
                if n == 0:
                    take_v_lo(j - 1, 1 - par, G - 1)
                for t in TAKE[n]:
                    if t >= 2 * C:
                        split_v(j, par, t - 2 * C)
                        if t > 2 * C:
                            take_v_lo(j, par, t - 2 * C - 1)
                if not masked and real(j) and n in (2, 4, 6, 8):
                    g = n // 2 - 1
                    pool.wait_ge(ph.hn_done, G * j + g + 1)
                    xg = ring(ph.x, j)[:, g, :]
                    nc.gpsimd.tensor_tensor(xg, xg, bo_rows[:], ALU.add).then_inc(xb_done, 1)

        pipeline(pool, quads, iteration)



def layer1_phase(nc, ctx, name, quads, consts, x_in, x_out, adj, weights, m0, first, b_lin, ln_a, ln_b, h_in=None):
    first_layer = h_in is None
    TILES = 3 + 3 + G
    PIECES = TILES * C
    ph = Phase(nc, ctx, name, quads, consts, x_in, x_out, adj, weights, m0, first, 3, norm=first_layer, h_in=h_in)
    ph.TILES = TILES
    sb, ps, sem, real = ph.sb, ph.ps, ph.sem, ph.real

    ps_u, ps_a, ps_e = ps("ps_u"), ps("ps_a"), ps("ps_e")
    ps_c = [ps(f"ps_c{i}") for i in range(2)]
    mT_hi, mT_lo = ([sb(f"mT_{half}{i}", [P, C, G, 2, P], F32R) for i in range(2)] for half in ("hi", "lo"))
    lin_hi, lin_lo = ([sb(f"lin_{half}{i}", [P, G, D], F32R) for i in range(2)] for half in ("hi", "lo"))
    w2 = [sb(f"w2_{i}", [P, G, 2, P], F32) for i in range(2)]
    uw, us = sb("uw", [P, 2, P], F32), sb("us", [P, P], F32)
    ex = [sb(f"ex{i}", [P, P], F32) for i in range(2)]
    at = [sb(f"at{i}", [P, P], F32) for i in range(2)]
    atT_hi, atT_lo = ([sb(f"atT_{half}{i}", [P, P], F32R) for i in range(2)] for half in ("hi", "lo"))
    cs = [sb(f"cs{i}", [P, G, D], F32) for i in range(2)]
    sums = [sb(f"sums{i}", [P, G], F32) for i in range(2)]
    cst = sb("cst", [P, G, 6], F32)
    cmom, cmean, cvar = sb("cmom", [P, 4, G], F32), sb("cmean", [P, G], F32), sb("cvar", [P, G], F32)
    sm = sb("sm", [P, 9, G], F32)
    bl_rows, a_rows, b_rows = (sb(n, [P, D], F32) for n in ("bl_rows", "a_rows", "b_rows"))

    m_hi_done, m_lo_done, lin_hi_done, lin_lo_done = (
        sem(n) for n in ("m_hi_done", "m_lo_done", "lin_hi_done", "lin_lo_done"))
    u_done, uw_done, us_done, ex_done = sem("u_done"), sem("uw_done"), sem("us_done"), sem("ex_done")
    at_done, at_turned, atT_hi_done = sem("at_done"), sem("at_turned"), sem("atT_hi_done")
    atT_lo_done = sem("atT_lo_done")
    adj_turned, w2_left, w2_right = sem("adj_turned"), sem("w2_left"), sem("w2_right")
    ctx_done, cs_made, cs_stats, cmom_step = sem("ctx_done"), sem("cs_made"), sem("cs_stats"), sem("cmom_step")
    relu_done = sem("relu_done")
    step, sigma_done, z_done, scaled, affine_done = (
        sem(n) for n in ("step", "sigma_done", "z_done", "scaled", "affine_done"))
    STEPS = 8
    PLAN = LAYER1_PLAN

    def wait_ps_t_free(pe, q, g):
        if due(G * q + g):
            pe.wait_ge(ph.hT_lo_done, G * q + g)
    ph.wait_ps_t_free = wait_ps_t_free

    def wait_hT_free(eng, q, g):
        if due(TILES * (q - 1)):
            eng.wait_ge(ph.proj_done, TILES * (q - 1))
        if due(G * (q - 2) + g + 1):
            eng.wait_ge(u_done, G * (q - 2) + g + 1)
    ph.wait_hT_free = wait_hT_free

    def pieces(n):
        return range(n * PIECES // SLOTS, (n + 1) * PIECES // SLOTS)

    TAKE = [[t for t in range(TILES) if C * t + C - 1 in pieces(n)] for n in range(SLOTS)]

    ph.clear_semaphores()
    block = ctx.enter_context(nc.Block())

    @block.sync
    def _(sp):
        def load_h(q, par):
            if not real(q):
                return
            if first_layer:
                if due(G * (q + 1 - RING)):
                    sp.wait_ge(ph.hn_done, G * (q + 1 - RING))
            else:
                if due(G * (q - 1)):
                    sp.wait_ge(ph.hT_turned, G * (q - 1))
            if not isinstance(q, int) or q >= 2:
                sp.wait_ge((ph.x_landed if first_layer else ph.h_landed)[par], dmas(q - 2, par))
            if first_layer:
                sp.dma_start(ring(ph.x, q), quad_of(x_in, q)).then_inc(ph.x_landed[par], 16)
            else:
                sp.dma_start(ph.hn[par][:], quad_of(h_in, q)).then_inc(ph.h_landed[par], 16)

        def store(q, par):
            if not real(q):
                return
            if first_layer and is_last(q, quads):
                ph.store_graphs(sp, q, par, affine_done, cs[par])
            elif first_layer:
                sp.wait_ge(affine_done, G * (q + 1))
                sp.dma_start(quad_of(x_out, q), cs[par][:]).then_inc(ph.stored[par], 16)
            else:
                ph.store_x(sp, q, par)

        ph.load_first_quad(sp)
        load_h(0, 0)
        ph.load_first(sp)
        for dst, b in ((bl_rows, b_lin), (a_rows, ln_a), (b_rows, ln_b)):
            sp.dma_start(dst[:], b.partition_broadcast(P)).then_inc(ph.rows_in, 16)

        def iteration(j, par):
            if not isinstance(j, int) or j >= 0:
                load_h(j + 1, 1 - par)
            if real(j):
                if due(G * (j - 1)):
                    sp.wait_ge(at_done, G * (j - 1))
                sp.dma_start(ph.adj[par][:], quad_of(adj, j)).then_inc(ph.adj_landed[par], 16)
            if not first_layer:
                ph.load_x(sp, j - 1, 1 - par)
            store(j - 3, 1 - par)
            ph.load_next(sp, j)

        pipeline(sp, quads, iteration, start=4)
        store(quads - 1, (quads - 1) % 2)
        ph.wait_stores(sp)

    @block.tensor
    def _(pe):

        def scores(q, par, g):
            if not real(q):
                return
            if g == 0:
                pe.wait_ge(m_hi_done, 2 * C * (q + 1))
                pe.wait_ge(m_lo_done, 2 * C * (q + 1))
            if due(G * q + g):
                pe.wait_ge(uw_done, G * q + g)
            mm, out = nc.tensor.matmul, ps_u[:, 0:2 * P]
            for c in range(C):
                hi, lo = (h[par][:, c, g * P:(g + 1) * P] for h in (ph.hT_hi, ph.hT_lo))
                mm(out, hi, mT_hi[par][:, c, g], start=(c == 0), stop=False)
                mm(out, hi, mT_lo[par][:, c, g], start=False, stop=False)
                last = mm(out, lo, mT_hi[par][:, c, g], start=False, stop=(c == C - 1))
            last.then_inc(u_done, 1)

        def project(j, par, k):
            if not real(j) or k >= PIECES:
                return
            t, c = k // C, k % C
            if k == 0:
                if isinstance(j, int) and j == 0:
                    ph.wait_weights(pe, 3)
                pe.wait_ge(ph.hT_hi_done, G * (j + 1))
                pe.wait_ge(ph.hT_lo_done, G * (j + 1))
            if c == 0:
                if t < 2:
                    if due(G * (j - 1) + 3 + t):
                        pe.wait_ge(lin_lo_done, G * (j - 1) + 3 + t)
                elif t < 8:
                    pe.wait_ge(m_lo_done, 2 * C * j + t - 1)
                else:
                    pe.wait_ge(lin_lo_done, G * j + t - 7)
            bank = ph.ps_proj[t % 2]
            if t < 2 * C:
                last = ph.project_turned(par, bank, t % 2, t // 2, c)
            else:
                last = ph.project_rows(par, bank, 2, t - 2 * C, c)
            if c == C - 1:
                last.then_inc(ph.proj_done, 1)

        def turn_adj(j, par):
            if not real(j):
                return
            pe.wait_ge(ph.adj_landed[par], dmas(j, par))
            if due(j):
                pe.wait_ge(w2_right, j)
            for g in range(G):
                last = nc.tensor.transpose(ps_a[:, g * P:(g + 1) * P], ph.adj[par][:, g, :], ph.ident[:])
            last.then_inc(adj_turned, 1)

        def turn_attention(q, g):
            if not real(q):
                return
            pe.wait_ge(at_done, G * q + g + 1)
            if due(G * q + g):
                pe.wait_ge(atT_lo_done, G * q + g)
            nc.tensor.transpose(ps_e[:, 0:P], at[g % 2][:], ph.ident[:]).then_inc(at_turned, 1)

        def context(q, par, g):
            if not real(q):
                return
            pe.wait_ge(atT_hi_done, G * q + g + 1)
            pe.wait_ge(atT_lo_done, G * q + g + 1)
            if g == 0:
                pe.wait_ge(lin_hi_done, G * (q + 1))
                pe.wait_ge(lin_lo_done, G * (q + 1))
            if due(G * q + g - 1):
                pe.wait_ge(cs_made, G * q + g - 1)
            mm, out = nc.tensor.matmul, ps_c[g % 2][:, 0:D]
            mm(out, atT_hi[g % 2][:], lin_hi[par][:, g, :], start=True, stop=False)
            mm(out, atT_hi[g % 2][:], lin_lo[par][:, g, :], start=False, stop=False)
            mm(out, atT_lo[g % 2][:], lin_hi[par][:, g, :], start=False, stop=True).then_inc(ctx_done, 1)

        def iteration(j, par):
            for n in range(SLOTS):
                for back, g in due_in(n, PLAN["scores"]):
                    scores(j - 1 - back, (par + 1 + back) % 2, g)
                for k in pieces(n):
                    project(j, par, k)
                for _, g in due_in(n, PLAN["h"]):
                    ph.turn_h(pe, j + 1, 1 - par, g)
                if n == PLAN["adj"]:
                    turn_adj(j, par)
                for back, g in due_in(n, PLAN["turn"]):
                    turn_attention(j - 1 - back, g)
                for back, g in due_in(n, PLAN["context"]):
                    context(j - 1 - back, (par + 1 + back) % 2, g)

        pipeline(pe, quads, iteration)

    @block.scalar
    def _(act):

        def take_m_hi(j, par, t):
            if not real(j):
                return
            act.wait_ge(ph.proj_done, TILES * j + t + 1)
            if t == 0:
                if due(G * (j - 1)):
                    act.wait_ge(u_done, G * (j - 1))
            nc.scalar.activation(mT_hi[par][:, t // 2, :, t % 2, :], graphs(ph.ps_proj[t % 2]), ACT.Identity)\
                .then_inc(m_hi_done, 1)

        def take_lin_hi(j, par, g):
            if not real(j):
                return
            t = 2 * C + g
            act.wait_ge(ph.proj_done, TILES * j + t + 1)
            if g == 0:
                if due(G * (j - 1)):
                    act.wait_ge(ctx_done, G * (j - 1))
            nc.scalar.activation(lin_hi[par][:, g, :], ph.ps_proj[t % 2][:, 0:D], ACT.Identity).then_inc(lin_hi_done, 1)

        def exponentials(q, g):
            if not real(q):
                return
            act.wait_ge(us_done, G * q + g + 1)
            if due(G * q + g - 1):
                act.wait_ge(at_done, G * q + g - 1)
            nc.scalar.activation(ex[g % 2][:], us[:], ACT.Exp, scale=float(D) ** -0.5).then_inc(ex_done, 1)

        def take_atT_hi(q, g):
            if not real(q):
                return
            act.wait_ge(at_turned, G * q + g + 1)
            if due(G * q + g - 1):
                act.wait_ge(ctx_done, G * q + g - 1)
            nc.scalar.activation(atT_hi[g % 2][:], ps_e[:, 0:P], ACT.Identity).then_inc(atT_hi_done, 1)

        def normalise(q, par, g):
            if not real(q) or is_last(q, quads):
                return
            if g == 0:
                act.wait_ge(step, STEPS * (q + 1))
            z = cs[par][:, g, :]
            nc.scalar.activation(z, z, ACT.Identity, bias=sm[:, 8, g:g + 1], scale=sm[:, 7, g:g + 1]).then_inc(z_done, 1)

        def relu_output(q, par, g):
            if first_layer or not real(q) or is_last(q, quads):
                return
            act.wait_ge(affine_done, G * q + g + 1)
            nc.scalar.activation(cs[par][:, g, :], cs[par][:, g, :], ACT.Relu).then_inc(relu_done, 1)

        def iteration(j, par):
            for n in range(SLOTS):
                ph.first_hi(act, j, n)
                ph.next_hi(act, j, n)
                for back, g in due_in(n, PLAN["exp"]):
                    exponentials(j - 1 - back, g)
                for back, g in due_in(n, PLAN["turn"]):
                    take_atT_hi(j - 1 - back, g)
                for t in TAKE[n]:
                    if t < 2 * C:
                        take_m_hi(j, par, t)
                    else:
                        take_lin_hi(j, par, t - 2 * C)
                for _, g in due_in(n, PLAN["apply"]):
                    ph.norm_apply(act, j + 1, g)
                for _, g in due_in(n, PLAN["h"]):
                    ph.take_hT_hi(act, j + 1, 1 - par, g)
                for _, g in due_in(n, PLAN["z"]):
                    normalise(j - 2, par, g)
                for _, g in due_in(n, PLAN["relu"]):
                    relu_output(j - 2, par, g)

        pipeline(act, quads, iteration)

    @block.vector
    def _(dve):

        def weigh_scores(q, par, g):
            if not real(q):
                return
            e = G * q + g
            if g == 0:
                dve.wait_ge(w2_left, q + 1)
                dve.wait_ge(w2_right, q + 1)
            dve.wait_ge(u_done, e + 1)
            if due(e):
                dve.wait_ge(us_done, e)
            nc.vector.tensor_tensor(uw[:], ps_u[:, 0:2 * P].rearrange("p (s n) -> p s n", s=2), w2[par][:, g], ALU.mult)\
                .then_inc(uw_done, 1)
            dve.wait_ge(uw_done, e + 1)
            if due(e):
                dve.wait_ge(ex_done, e)
            nc.vector.tensor_tensor(us[:], uw[:, 0, :], uw[:, 1, :], ALU.add).then_inc(us_done, 1)

        def weigh_exponentials(q, par, g):
            if not real(q):
                return
            e = G * q + g
            dve.wait_ge(ex_done, e + 1)
            if due(e - 1):
                dve.wait_ge(at_turned, e - 1)
            if g == 0:
                if due(STEPS * (q - 1)):
                    dve.wait_ge(step, STEPS * (q - 1))
            nc.vector.tensor_tensor_reduce(out=at[g % 2][:], in0=ex[g % 2][:], in1=ph.adj[par][:, g, :], scale=1.0,
                                           scalar=0.0, op0=ALU.mult, op1=ALU.add, accum_out=sums[par][:, g:g + 1])\
                .then_inc(at_done, 1)

        def take_m_lo(j, par, t):
            if not real(j):
                return
            dve.wait_ge(m_hi_done, 2 * C * j + t + 1)
            nc.vector.tensor_tensor(mT_lo[par][:, t // 2, :, t % 2, :], graphs(ph.ps_proj[t % 2]),
                                    mT_hi[par][:, t // 2, :, t % 2, :].bitcast(F32), ALU.subtract).then_inc(m_lo_done, 1)

        def take_lin_lo(j, par, g):
            if not real(j):
                return
            dve.wait_ge(lin_hi_done, G * j + g + 1)
            nc.vector.tensor_tensor(lin_lo[par][:, g, :], ph.ps_proj[g % 2][:, 0:D], lin_hi[par][:, g, :].bitcast(F32),
                                    ALU.subtract).then_inc(lin_lo_done, 1)

        def take_atT_lo(q, g):
            if not real(q):
                return
            dve.wait_ge(atT_hi_done, G * q + g + 1)
            nc.vector.tensor_tensor(atT_lo[g % 2][:], ps_e[:, 0:P], atT_hi[g % 2][:].bitcast(F32), ALU.subtract)\
                .then_inc(atT_lo_done, 1)

        def right_weights(j, par):
            if not real(j):
                return
            dve.wait_ge(adj_turned, j + 1)
            if due(G * (j - 1)):
                dve.wait_ge(uw_done, G * (j - 1))
            nc.vector.tensor_tensor(w2[par][:, :, 1, :], ps_a[:].rearrange("p (g n) -> p g n", g=G),
                                    over(consts["below"][:], G, 1), ALU.mult).then_inc(w2_right, 1)

        def take_context(q, par, g):
            if not real(q):
                return
            e = G * q + g
            dve.wait_ge(ctx_done, e + 1)
            dve.wait_ge(at_done, e + 1)
            if g == 0:
                if first_layer and (not isinstance(q, int) or q >= 2):
                    dve.wait_ge(ph.stored[par], dmas(q - 2, par))
                elif not first_layer:
                    if due(G * (q - 1)):
                        dve.wait_ge(ph.x_done, G * (q - 1))
            nc.vector.scalar_tensor_tensor(out=cs[par][:, g, :], in0=bl_rows[:], scalar=sums[par][:, g:g + 1],
                                           in1=ps_c[g % 2][:, 0:D], op0=ALU.mult, op1=ALU.add).then_inc(cs_made, 1)
            dve.wait_ge(cs_made, e + 1)
            nc.vector.bn_stats(cst[:, g, :], cs[par][:, g, :]).then_inc(cs_stats, 1)

        def close_rows(q, par, part):
            if not real(q):
                return
            v = nc.vector
            if part == 0:
                moments(v, dve, cs_stats, G * (q + 1), cst, cmom, cmean, cvar, cmom_step, q)
                v.tensor_scalar(sm[:, 0], sums[par][:], 1e-10, None, ALU.add).then_inc(step, 1)
                dve.wait_ge(step, STEPS * q + 1)
                v.reciprocal(sm[:, 1], sm[:, 0]).then_inc(step, 1)
                dve.wait_ge(step, STEPS * q + 2)
                v.tensor_tensor(sm[:, 2], sm[:, 1], sm[:, 1], ALU.mult).then_inc(step, 1)
                dve.wait_ge(step, STEPS * q + 3)
                if due(q):
                    dve.wait_ge(sigma_done, q)
                v.scalar_tensor_tensor(out=sm[:, 3], in0=cvar[:], scalar=float(D) / (D - 1), in1=sm[:, 2],
                                       op0=ALU.mult, op1=ALU.mult).then_inc(step, 1)
            else:
                dve.wait_ge(sigma_done, q + 1)
                v.tensor_scalar(sm[:, 5], sm[:, 4], 1e-3, None, ALU.add).then_inc(step, 1)
                dve.wait_ge(step, STEPS * q + 5)
                v.reciprocal(sm[:, 6], sm[:, 5]).then_inc(step, 1)
                dve.wait_ge(step, STEPS * q + 6)
                if due(G * q):
                    dve.wait_ge(z_done, G * q)
                v.tensor_tensor(sm[:, 7], sm[:, 6], sm[:, 1], ALU.mult).then_inc(step, 1)
                dve.wait_ge(step, STEPS * q + 7)
                v.scalar_tensor_tensor(out=sm[:, 8], in0=cmean[:], scalar=-1.0, in1=sm[:, 7], op0=ALU.mult, op1=ALU.mult)\
                    .then_inc(step, 1)

        def normalise_last(q, par, g):
            if not is_last(q, quads):
                return
            z = cs[par][:, g, :]
            if g == 0:
                dve.wait_ge(affine_done, G * q)
            nc.vector.scalar_tensor_tensor(out=z, in0=z, scalar=cmean[:, g:g + 1], in1=a_rows[:], op0=ALU.subtract,
                                           op1=ALU.mult).then_inc(scaled, 1)
            dve.wait_ge(scaled, G * q + g + 1)
            nc.vector.scalar_tensor_tensor(out=z, in0=z, scalar=sm[:, 7, g:g + 1], in1=b_rows[:], op0=ALU.mult,
                                           op1=ALU.add).then_inc(affine_done, 1)

        def add_last_output(q, par, g):
            if first_layer or not is_last(q, quads):
                return
            if g == 0:
                dve.wait_ge(ph.x_done, G * q)
                dve.wait_ge(ph.x_landed[par], dmas(q, par))
            dve.wait_ge(affine_done, G * q + g + 1)
            xg = ring(ph.x, q)[:, g, :]
            nc.vector.scalar_tensor_tensor(out=xg, in0=cs[par][:, g, :], scalar=0.0, in1=xg, op0=ALU.max, op1=ALU.add)\
                .then_inc(ph.x_done, 1)

        def iteration(j, par):
            if isinstance(j, int) and j == 0:
                dve.wait_ge(ph.rows_in, 48)
            for n in range(SLOTS):
                ph.first_lo(dve, j, n)
                ph.next_lo(dve, j, n)
                for back, g in due_in(n, PLAN["weigh"]):
                    weigh_scores(j - 1 - back, (par + 1 + back) % 2, g)
                for back, g in due_in(n, PLAN["at"]):
                    weigh_exponentials(j - 1 - back, (par + 1 + back) % 2, g)
                for back, g in due_in(n, PLAN["atT_lo"]):
                    take_atT_lo(j - 1 - back, g)
                for t in TAKE[n]:
                    if t < 2 * C:
                        take_m_lo(j, par, t)
                    else:
                        take_lin_lo(j, par, t - 2 * C)
                for part in range(2):
                    if n == PLAN["close"][part]:
                        close_rows(j - 2, par, part)
                for _, g in due_in(n, PLAN["z"]):
                    normalise_last(j - 2, par, g)
                for _, g in due_in(n, PLAN["stats"]):
                    ph.norm_stats(dve, j + 1, 1 - par, g)
                if n == PLAN["eps"]:
                    ph.norm_eps(dve, j + 1)
                if n == PLAN["right"]:
                    right_weights(j, par)
                for _, g in due_in(n, PLAN["h"]):
                    ph.take_hT_lo(dve, j + 1, 1 - par, g)
                for back, g in due_in(n, PLAN["cs"]):
                    take_context(j - 1 - back, (par + 1 + back) % 2, g)
                for _, g in due_in(n, PLAN["x"]):
                    add_last_output(j - 2, par, g)

        pipeline(dve, quads, iteration)

    @block.gpsimd
    def _(pool):
        def add_output(q, par, g):
            if first_layer:
                return
            if g == 0:
                pool.wait_ge(ph.x_landed[par], dmas(q, par))
            pool.wait_ge(relu_done, G * q + g + 1)
            xg = ring(ph.x, q)[:, g, :]
            nc.gpsimd.tensor_tensor(xg, cs[par][:, g, :], xg, ALU.add).then_inc(ph.x_done, 1)

        def iteration(j, par):
            if isinstance(j, int) and j == 0:
                pool.wait_ge(ph.rows_in, 48)
            if real(j - 2):
                pool.wait_ge(step, STEPS * (j - 2) + 4)
                nc.gpsimd.tensor_tensor(sm[:, 4], sm[:, 3], consts["neg_half"][:, G:2 * G], ALU.pow)\
                    .then_inc(sigma_done, 1)
            ph.norm_rstd(pool, j + 1)
            if real(j):
                pool.wait_ge(ph.adj_landed[par], dmas(j, par))
                if due(G * (j - 1)):
                    pool.wait_ge(uw_done, G * (j - 1))
                nc.gpsimd.tensor_tensor(w2[par][:, :, 0, :], ph.adj[par][:], over(consts["above"][:], G, 1), ALU.mult)\
                    .then_inc(w2_left, 1)
            if real(j - 2) and not is_last(j - 2, quads):
                for g in range(G):
                    z, e = cs[par][:, g, :], G * (j - 2) + g
                    pool.wait_ge(z_done, e + 1)
                    nc.gpsimd.tensor_tensor(z, z, a_rows[:], ALU.mult).then_inc(scaled, 1)
                    pool.wait_ge(scaled, e + 1)
                    nc.gpsimd.tensor_tensor(z, z, b_rows[:], ALU.add).then_inc(affine_done, 1)
                    if g > 0:
                        add_output(j - 2, par, g - 1)
                add_output(j - 2, par, G - 1)

        pipeline(pool, quads, iteration)


def layer2_phase(nc, ctx, name, quads, consts, x_in, x_out, adj, weights, m0, first, b_left, b_self, b_right, gamma,
                 beta):
    TILES = 3 * G
    PIECES = TILES * C
    ph = Phase(nc, ctx, name, quads, consts, x_in, x_out, adj, weights, m0, first, 3, ring_quads=6)
    ph.TILES = TILES
    sb, ps, sem, real = ph.sb, ph.ps, ph.sem, ph.real
    SCALE = float(D) ** -0.5

    def pieces(n):
        return range(n * PIECES // SLOTS, (n + 1) * PIECES // SLOTS)

    TAKE = [[t for t in range(TILES) if C * t + C - 1 in pieces(n)] for n in range(SLOTS)]

    ps_u, ps_e = ps("ps_u"), ps("ps_e")
    ps_c = [ps(f"ps_c{i}") for i in range(2)]
    hT = [sb(f"hT{i}", [P, C, G * P], F32) for i in range(2)]
    lin = [sb(f"lin{i}", [P, G, 3, D], F32) for i in range(2)]
    nmax, nms = sb("nmax", [P, 1], F32), sb("nms", [P, 1], F32)
    ex = [sb(f"ex{i}", [P, P], F32) for i in range(2)]
    at = [sb(f"at{i}", [P, P], F32) for i in range(2)]
    junk = sb("junk", [P, P], F32)
    atT = [sb(f"atT{i}", [P, 2, P], F32) for i in range(2)]
    cs = [sb(f"cs{i}", [P, G, D], F32) for i in range(2)]
    esum, asum, diag = ([sb(f"{n}{i}", [P, G], F32) for i in range(2)] for n in ("esum", "asum", "diag"))
    cst = sb("cst", [P, G, 6], F32)
    cmom, cmean, cvar = sb("cmom", [P, 4, G], F32), sb("cmean", [P, G], F32), sb("cvar", [P, G], F32)
    sm = sb("sm", [P, 11, G], F32)
    b_rows = sb("b_rows", [P, 3, D], F32)
    gamma_rows, beta_rows = sb("gamma_rows", [P, D], F32), sb("beta_rows", [P, D], F32)

    hT_done = ph.hT_acted = sem("hT_done")
    lin_taken = sem("lin_taken")
    u_done, nmax_done, nms_done, ex_done = sem("u_done"), sem("nmax_done"), sem("nms_done"), sem("ex_done")
    at_done, diag_done, at_turned, atT_done = sem("at_done"), sem("diag_done"), sem("at_turned"), sem("atT_done")
    ctx_done, cs_made, cs_stats, cmom_step = sem("ctx_done"), sem("cs_made"), sem("cs_stats"), sem("cmom_step")
    relu_done = sem("relu_done")
    step, rsig_done, z_done, scaled, affine_done = (
        sem(n) for n in ("step", "rsig_done", "z_done", "scaled", "affine_done"))
    STEPS = 10
    PLAN = LAYER2_PLAN

    def wait_ps_t_free(pe, q, g):
        if due(G * q + g):
            pe.wait_ge(ph.hT_lo_done, G * q + g)
        if due(G * q + g):
            pe.wait_ge(hT_done, G * q + g)
    ph.wait_ps_t_free = wait_ps_t_free

    ph.clear_semaphores()
    block = ctx.enter_context(nc.Block())

    @block.sync
    def _(sp):
        ph.load_first_quad(sp)
        ph.load_x(sp, 0, 0)
        ph.load_first(sp)
        for dst, b in ((b_rows[:, 0], b_left), (b_rows[:, 1], b_self), (b_rows[:, 2], b_right), (gamma_rows[:], gamma),
                       (beta_rows[:], beta)):
            sp.dma_start(dst, b.partition_broadcast(P)).then_inc(ph.rows_in, 16)

        def iteration(j, par):
            ph.load_x(sp, j + 2, par)
            if real(j):
                if due(G * (j - 1)):
                    sp.wait_ge(at_done, G * (j - 1))
                sp.dma_start(ph.adj[par][:], quad_of(adj, j)).then_inc(ph.adj_landed[par], 16)
            ph.store_x(sp, j - 3, 1 - par)
            ph.load_next(sp, j)

        pipeline(sp, quads, iteration, start=4)
        ph.store_x(sp, quads - 1, (quads - 1) % 2)
        ph.wait_stores(sp)

    @block.tensor
    def _(pe):

        def scores(q, par, g):
            if not real(q):
                return
            if g == 0:
                pe.wait_ge(hT_done, G * (q + 1))
            if due(G * q + g):
                pe.wait_ge(ex_done, G * q + g)
            if due(G * q + g):
                pe.wait_ge(nmax_done, G * q + g)
            for c in range(C):
                hg = hT[par][:, c, g * P:(g + 1) * P]
                last = nc.tensor.matmul(ps_u[:, 0:P], hg, hg, start=(c == 0), stop=(c == C - 1))
            last.then_inc(u_done, 1)

        def project(j, par, k):
            if not real(j):
                return
            t, c = k // C, k % C
            if k == 0:
                if isinstance(j, int) and j == 0:
                    ph.wait_weights(pe, 3)
                pe.wait_ge(ph.hT_hi_done, G * (j + 1))
                pe.wait_ge(ph.hT_lo_done, G * (j + 1))
            if c == 0:
                if due(TILES * j + t - 1):
                    pe.wait_ge(lin_taken, TILES * j + t - 1)
            last = ph.project_rows(par, ph.ps_proj[t % 2], t % 3, t // 3, c)
            if c == C - 1:
                last.then_inc(ph.proj_done, 1)

        def turn_attention(q, g):
            if not real(q):
                return
            pe.wait_ge(at_done, G * q + g + 1)
            if due(G * q + g):
                pe.wait_ge(atT_done, G * q + g)
            nc.tensor.transpose(ps_e[:, 0:P], at[g % 2][:], ph.ident[:]).then_inc(at_turned, 1)

        def context(q, par, g):
            if not real(q):
                return
            pe.wait_ge(atT_done, G * q + g + 1)
            if g == 0:
                pe.wait_ge(lin_taken, TILES * (q + 1))
            if due(G * q + g - 1):
                pe.wait_ge(cs_made, G * q + g - 1)
            out = ps_c[g % 2][:, 0:D]
            nc.tensor.matmul(out, atT[g % 2][:, 0, :], lin[par][:, g, 0, :], start=True, stop=False)
            nc.tensor.matmul(out, atT[g % 2][:, 1, :], lin[par][:, g, 2, :], start=False, stop=True)\
                .then_inc(ctx_done, 1)

        def iteration(j, par):
            for n in range(SLOTS):
                for back, g in due_in(n, PLAN["scores"]):
                    scores(j - 1 - back, (par + 1 + back) % 2, g)
                for k in pieces(n):
                    project(j, par, k)
                for _, g in due_in(n, PLAN["h"]):
                    ph.turn_h(pe, j + 1, 1 - par, g)
                for back, g in due_in(n, PLAN["turn"]):
                    turn_attention(j - 1 - back, g)
                for back, g in due_in(n, PLAN["context"]):
                    context(j - 1 - back, (par + 1 + back) % 2, g)

        pipeline(pe, quads, iteration)

    @block.scalar
    def _(act):

        def take_hT(q, par, g):
            if not real(q):
                return
            if due(G * (q - 2) + g + 1):
                act.wait_ge(u_done, G * (q - 2) + g + 1)
            nc.scalar.activation(hT[par][:, :, g * P:(g + 1) * P], chunks(ph.bank_of_h(q, g)), ACT.Relu)\
                .then_inc(hT_done, 1)

        def exponentials(q, par, g):
            if not real(q):
                return
            act.wait_ge(nms_done, G * q + g + 1)
            if due(G * q + g - 1):
                act.wait_ge(at_done, G * q + g - 1)
            if g == 0:
                if due(STEPS * (q - 1)):
                    act.wait_ge(step, STEPS * (q - 1))
            nc.scalar.activation(ex[g % 2][:], ps_u[:, 0:P], ACT.Exp, bias=nms[:, 0:1], scale=SCALE,
                                 accum_out=esum[par][:, g:g + 1]).then_inc(ex_done, 1)

        def normalise(q, par, g):
            if not real(q) or is_last(q, quads):
                return
            if g == 0:
                act.wait_ge(step, STEPS * (q + 1))
            z = cs[par][:, g, :]
            nc.scalar.activation(z, z, ACT.Identity, bias=sm[:, 10, g:g + 1], scale=sm[:, 9, g:g + 1]).then_inc(z_done, 1)

        def relu_output(q, par, g):
            if not real(q) or is_last(q, quads):
                return
            act.wait_ge(affine_done, G * q + g + 1)
            nc.scalar.activation(cs[par][:, g, :], cs[par][:, g, :], ACT.Relu).then_inc(relu_done, 1)

        def iteration(j, par):
            for n in range(SLOTS):
                ph.first_hi(act, j, n)
                ph.next_hi(act, j, n)
                for back, g in due_in(n, PLAN["exp"]):
                    exponentials(j - 1 - back, (par + 1 + back) % 2, g)
                for _, g in due_in(n, PLAN["apply"]):
                    ph.norm_apply(act, j + 1, g)
                for _, g in due_in(n, PLAN["h"]):
                    ph.take_hT_hi(act, j + 1, 1 - par, g)
                    take_hT(j + 1, 1 - par, g)
                for _, g in due_in(n, PLAN["z"]):
                    normalise(j - 2, par, g)
                for _, g in due_in(n, PLAN["relu"]):
                    relu_output(j - 2, par, g)

        pipeline(act, quads, iteration)

    @block.vector
    def _(dve):

        def row_maxima(q, g):
            if not real(q):
                return
            e = G * q + g
            dve.wait_ge(u_done, e + 1)
            if due(e):
                dve.wait_ge(ex_done, e)
            nc.vector.tensor_reduce(nmax[:], ps_u[:, 0:P], AX.X, ALU.max, negate=True).then_inc(nmax_done, 1)
            dve.wait_ge(nmax_done, e + 1)
            nc.vector.tensor_scalar(nms[:], nmax[:], SCALE, None, ALU.mult).then_inc(nms_done, 1)

        def weigh_exponentials(q, par, g):
            if not real(q):
                return
            e = G * q + g
            if g == 0:
                dve.wait_ge(ph.adj_landed[par], dmas(q, par))
            dve.wait_ge(ex_done, e + 1)
            if due(e - 1):
                dve.wait_ge(at_turned, e - 1)
            nc.vector.tensor_tensor_reduce(out=at[g % 2][:], in0=ex[g % 2][:], in1=ph.adj[par][:, g, :], scale=1.0,
                                           scalar=0.0, op0=ALU.mult, op1=ALU.add, accum_out=asum[par][:, g:g + 1])\
                .then_inc(at_done, 1)
            dve.wait_ge(at_done, e + 1)
            if due(e):
                dve.wait_ge(diag_done, e)
            nc.vector.tensor_tensor_reduce(out=junk[:], in0=at[g % 2][:], in1=ph.ident[:], scale=1.0,
                                           scalar=0.0, op0=ALU.mult, op1=ALU.add, accum_out=diag[par][:, g:g + 1])\
                .then_inc(diag_done, 1)

        def split_attention(q, g):
            if not real(q):
                return
            e = G * q + g
            dve.wait_ge(at_turned, e + 1)
            if due(e - 1):
                dve.wait_ge(ctx_done, e - 1)
            nc.vector.tensor_tensor(atT[g % 2][:], over(ps_e[:, 0:P], 2, 1), consts["sides"][:], ALU.mult)\
                .then_inc(atT_done, 1)

        def take_lin(j, par, t):
            if not real(j):
                return
            dve.wait_ge(ph.proj_done, TILES * j + t + 1)
            if t == 0:
                if due(G * (j - 1)):
                    dve.wait_ge(ctx_done, G * (j - 1))
            nc.vector.tensor_tensor(lin[par][:, t // 3, t % 3, :], ph.ps_proj[t % 2][:, 0:D], b_rows[:, t % 3, :],
                                    ALU.add).then_inc(lin_taken, 1)

        def take_context(q, par, g):
            if not real(q):
                return
            e = G * q + g
            dve.wait_ge(ctx_done, e + 1)
            dve.wait_ge(diag_done, e + 1)
            if g == 0:
                if due(G * (q - 1)):
                    dve.wait_ge(ph.x_done, G * (q - 1))
                dve.wait_ge(lin_taken, TILES * (q + 1))
            nc.vector.scalar_tensor_tensor(out=cs[par][:, g, :], in0=lin[par][:, g, 1, :], scalar=diag[par][:, g:g + 1],
                                           in1=ps_c[g % 2][:, 0:D], op0=ALU.mult, op1=ALU.add).then_inc(cs_made, 1)
            dve.wait_ge(cs_made, e + 1)
            nc.vector.bn_stats(cst[:, g, :], cs[par][:, g, :]).then_inc(cs_stats, 1)

        def close_rows(q, par, part):
            if not real(q):
                return
            v, s = nc.vector, STEPS * q
            if part == 0:
                moments(v, dve, cs_stats, G * (q + 1), cst, cmom, cmean, cvar, cmom_step, q)
                v.reciprocal(sm[:, 0], esum[par][:]).then_inc(step, 1)
                dve.wait_ge(step, s + 1)
                v.tensor_tensor(sm[:, 1], asum[par][:], sm[:, 0], ALU.mult).then_inc(step, 1)
                dve.wait_ge(step, s + 2)
                v.tensor_scalar(sm[:, 2], sm[:, 1], 1e-10, None, ALU.add).then_inc(step, 1)
                dve.wait_ge(step, s + 3)
                v.reciprocal(sm[:, 3], sm[:, 2]).then_inc(step, 1)
                dve.wait_ge(step, s + 4)
                v.tensor_tensor(sm[:, 4], sm[:, 3], sm[:, 0], ALU.mult).then_inc(step, 1)
                dve.wait_ge(step, s + 5)
                v.tensor_tensor(sm[:, 5], sm[:, 4], sm[:, 4], ALU.mult).then_inc(step, 1)
                dve.wait_ge(step, s + 6)
                v.tensor_tensor(sm[:, 6], cvar[:], sm[:, 5], ALU.mult).then_inc(step, 1)
                dve.wait_ge(step, s + 7)
                if due(q):
                    dve.wait_ge(rsig_done, q)
                v.tensor_scalar(sm[:, 7], sm[:, 6], 1e-12, None, ALU.add).then_inc(step, 1)
            else:
                dve.wait_ge(rsig_done, q + 1)
                if due(G * q):
                    dve.wait_ge(z_done, G * q)
                v.tensor_tensor(sm[:, 9], sm[:, 8], sm[:, 4], ALU.mult).then_inc(step, 1)
                dve.wait_ge(step, s + 9)
                v.scalar_tensor_tensor(out=sm[:, 10], in0=cmean[:], scalar=-1.0, in1=sm[:, 9], op0=ALU.mult, op1=ALU.mult)\
                    .then_inc(step, 1)

        def normalise_last(q, par, g):
            if not is_last(q, quads):
                return
            z = cs[par][:, g, :]
            if g == 0:
                dve.wait_ge(affine_done, G * q)
            nc.vector.scalar_tensor_tensor(out=z, in0=z, scalar=cmean[:, g:g + 1], in1=gamma_rows[:], op0=ALU.subtract,
                                           op1=ALU.mult).then_inc(scaled, 1)
            dve.wait_ge(scaled, G * q + g + 1)
            nc.vector.scalar_tensor_tensor(out=z, in0=z, scalar=sm[:, 9, g:g + 1], in1=beta_rows[:], op0=ALU.mult,
                                           op1=ALU.add).then_inc(affine_done, 1)

        def add_last_output(q, par, g):
            if not is_last(q, quads):
                return
            if g == 0:
                dve.wait_ge(ph.x_done, G * q)
            dve.wait_ge(affine_done, G * q + g + 1)
            xg = ring(ph.x, q)[:, g, :]
            nc.vector.scalar_tensor_tensor(out=xg, in0=cs[par][:, g, :], scalar=0.0, in1=xg, op0=ALU.max, op1=ALU.add)\
                .then_inc(ph.x_done, 1)

        def iteration(j, par):
            if isinstance(j, int) and j == 0:
                dve.wait_ge(ph.rows_in, 80)
            for n in range(SLOTS):
                ph.first_lo(dve, j, n)
                ph.next_lo(dve, j, n)
                for back, g in due_in(n, PLAN["exp"]):
                    row_maxima(j - 1 - back, g)
                for back, g in due_in(n, PLAN["at"]):
                    weigh_exponentials(j - 1 - back, (par + 1 + back) % 2, g)
                for back, g in due_in(n, PLAN["atT"]):
                    split_attention(j - 1 - back, g)
                for t in TAKE[n]:
                    take_lin(j, par, t)
                for part in range(2):
                    if n == PLAN["close"][part]:
                        close_rows(j - 2, par, part)
                for _, g in due_in(n, PLAN["z"]):
                    normalise_last(j - 2, par, g)
                for _, g in due_in(n, PLAN["stats"]):
                    ph.norm_stats(dve, j + 1, 1 - par, g)
                if n == PLAN["eps"]:
                    ph.norm_eps(dve, j + 1)
                for _, g in due_in(n, PLAN["h"]):
                    ph.take_hT_lo(dve, j + 1, 1 - par, g)
                for back, g in due_in(n, PLAN["cs"]):
                    take_context(j - 1 - back, (par + 1 + back) % 2, g)
                for _, g in due_in(n, PLAN["x"]):
                    add_last_output(j - 2, par, g)

        pipeline(dve, quads, iteration)

    @block.gpsimd
    def _(pool):
        def add_output(q, par, g):
            if g == 0:
                pool.wait_ge(ph.x_landed[par], dmas(q, par))
            pool.wait_ge(relu_done, G * q + g + 1)
            xg = ring(ph.x, q)[:, g, :]
            nc.gpsimd.tensor_tensor(xg, cs[par][:, g, :], xg, ALU.add).then_inc(ph.x_done, 1)

        def iteration(j, par):
            if isinstance(j, int) and j == 0:
                pool.wait_ge(ph.rows_in, 80)
            if real(j - 2):
                pool.wait_ge(step, STEPS * (j - 2) + 8)
                nc.gpsimd.tensor_tensor(sm[:, 8], sm[:, 7], consts["neg_half"][:, 0:G], ALU.pow).then_inc(rsig_done, 1)
            ph.norm_rstd(pool, j + 1)
            if real(j - 2) and not is_last(j - 2, quads):
                for g in range(G):
                    z, e = cs[par][:, g, :], G * (j - 2) + g
                    pool.wait_ge(z_done, e + 1)
                    nc.gpsimd.tensor_tensor(z, z, gamma_rows[:], ALU.mult).then_inc(scaled, 1)
                    pool.wait_ge(scaled, e + 1)
                    nc.gpsimd.tensor_tensor(z, z, beta_rows[:], ALU.add).then_inc(affine_done, 1)
                    if g > 0:
                        add_output(j - 2, par, g - 1)
                add_output(j - 2, par, G - 1)

        pipeline(pool, quads, iteration)


def build(nc, t, out, quads=16, phases=("l0", "l1a", "l1b", "l2", "l3")):
    with ExitStack() as top:
        consts = {}
        ident = consts["ident"] = top.enter_context(nc.sbuf_tensor("ident", [P, P], F32))
        neg_half = consts["neg_half"] = top.enter_context(nc.sbuf_tensor("neg_half", [P, 2 * G], F32))
        ones = top.enter_context(nc.sbuf_tensor("ones", [P, P], F32))
        above = consts["above"] = top.enter_context(nc.sbuf_tensor("above", [P, P], F32))
        below = consts["below"] = top.enter_context(nc.sbuf_tensor("below", [P, P], F32))
        sides = consts["sides"] = top.enter_context(nc.sbuf_tensor("sides", [P, 2, P], F32))
        zeroed = top.enter_context(nc.semaphore("zeroed"))
        with nc.Block() as block:
            @block.gpsimd
            def _(pool):
                nc.gpsimd.memset(ident[:], 0.0).then_inc(zeroed, 1)
                nc.gpsimd.memset(neg_half[:, 0:G], -0.5)
                nc.gpsimd.memset(neg_half[:, G:2 * G], 0.5)
                pool.wait_ge(zeroed, 1)
                nc.gpsimd.memset(ones[:], 1.0).then_inc(zeroed, 1)
                nc.gpsimd.affine_select(out=ident[:], in_=ident[:], compare_op=ALU.not_equal, fill=1.0, base=0,
                                        pattern=[[-1, P]], channel_multiplier=1)
                pool.wait_ge(zeroed, 2)
                for out_, base, sign in ((above[:], 0, 1), (below[:], -1, -1), (sides[:, 0], -1, -1), (sides[:, 1], -1, 1)):
                    nc.gpsimd.affine_select(out=out_, in_=ones[:], compare_op=ALU.is_ge, fill=0.0, base=base,
                                            pattern=[[sign, P]], channel_multiplier=-sign)
        x = t["x"]
        mid = [nc.dram_tensor(f"mid{i}", list(x.shape), F32, kind="Internal").ap() for i in range(3)]
        h_mid = nc.dram_tensor("h_mid", list(x.shape), F32, kind="Internal").ap()
        layer1 = [[t[f"L1_gnn_{n}"][l] for n in ("W_left_t", "W_right_t", "W_lin_t", "b_lin", "ln_a", "ln_b")]
                  for l in range(2)]
        matrices = dict(l0=[t[f"L0_gnn_W{n}"] for n in "qkv"], l1a=layer1[0][:3], l1b=layer1[1][:3],
                        l2=[t[f"L2_gnn_W_{n}_t"] for n in ("left", "self", "right")],
                        l3=[t[f"L3_gnn_W{n}_t"] for n in "qkvo"])
        weights = Weights(nc, top, [w for phase in phases for w in matrices[phase]])
        m0, start = {}, 0
        for phase in phases:
            m0[phase] = start
            start += len(matrices[phase])
        before = dict(l0=x, l1a=mid[0], l1b=None, l2=mid[1], l3=mid[2])
        quad = FirstQuad(nc, top, [x if k == 0 else before[phase] for k, phase in enumerate(phases)])
        first = {phase: (quad, k) for k, phase in enumerate(phases)}
        if "l0" in phases:
            with ExitStack() as ctx:
                attention_phase(nc, ctx, "l0", quads, consts, x, out if phases[-1] == "l0" else mid[0], t["adj"],
                                weights, m0["l0"], first["l0"], t["L0_gnn_bv"], bq=t["L0_gnn_bq"], bk=t["L0_gnn_bk"],
                                beta=t["L0_gnn_beta"], q_scale=float(HD) ** -0.5)
        if "l1b" in phases:
            src = x if phases[0] == "l1a" else mid[0]
            dst = out if phases[-1] == "l1b" else mid[1]
            with ExitStack() as ctx:
                layer1_phase(nc, ctx, "l1a", quads, consts, src, h_mid, t["adj"], weights, m0["l1a"], first["l1a"], *layer1[0][3:])
            with ExitStack() as ctx:
                layer1_phase(nc, ctx, "l1b", quads, consts, src, dst, t["adj"], weights, m0["l1b"], first["l1b"], *layer1[1][3:],
                             h_in=h_mid)
        if "l2" in phases:
            with ExitStack() as ctx:
                layer2_phase(nc, ctx, "l2", quads, consts, x if phases[0] == "l2" else mid[1],
                             out if phases[-1] == "l2" else mid[2], t["adj"], weights, m0["l2"], first["l2"],
                             *(t[f"L2_gnn_{n}"] for n in ("b_left", "b_self", "b_right", "gamma", "beta")))
        if "l3" in phases:
            with ExitStack() as ctx:
                attention_phase(nc, ctx, "l3", quads, consts, x if phases[0] == "l3" else mid[2], out, t["adj"],
                                weights, m0["l3"], first["l3"], t["L3_gnn_bv"], bo=t["L3_gnn_bo"], q_scale=float(D) ** -0.5)


_TURNED = ["L1_gnn_W_left", "L1_gnn_W_right", "L1_gnn_W_lin", "L2_gnn_W_left", "L2_gnn_W_self", "L2_gnn_W_right",
           "L3_gnn_Wq", "L3_gnn_Wk", "L3_gnn_Wv", "L3_gnn_Wo"]


def host_layout(inputs):
    import numpy as _np
    laid = {}
    for name, a in inputs.items():
        a = _np.asarray(a)
        if name in _TURNED:
            laid[name + "_t"] = _np.ascontiguousarray(_np.swapaxes(a, -1, -2))
        else:
            laid[name] = _np.ascontiguousarray(a.reshape(1) if a.ndim == 0 else a)
    return laid


def kernel(**inputs):
    import concourse.bacc as _bacc
    from concourse import mybir as _mybir
    from concourse.bass_utils import run_bass_kernel_spmd as _run

    laid = host_layout(inputs)
    nc = _bacc.Bacc("TRN2", target_bir_lowering=False, num_devices=1)
    arrays = {f"in_{name}_dram": a for name, a in laid.items()}
    handles = {name: nc.dram_tensor(f"in_{name}_dram", a.shape, _mybir.dt.from_np(a.dtype), kind="ExternalInput").ap()
               for name, a in laid.items()}
    out = nc.dram_tensor("out_0_dram", laid["x"].shape, _mybir.dt.from_np(laid["x"].dtype), kind="ExternalOutput").ap()
    build(nc, handles, out, quads=laid["x"].shape[0] // G)
    r = _run(nc, [arrays], core_ids=[0])
    return r.results[0]["out_0_dram"]
```
